# Optimizing a Trainium2 kernel written in Bass

```python
import numpy as np
import jax
import jax.numpy as jnp

def _softmax(x, axis=-1):
    return jax.nn.softmax(x, axis=axis)

def _gelu(x):
    return jax.nn.gelu(x, approximate=True)

def _silu(x):
    return jax.nn.silu(x)

def _sigmoid(x):
    return jax.nn.sigmoid(x)

def _layernorm(x, axis=-1, eps=1e-05):
    m = jnp.mean(x, axis=axis, keepdims=True)
    v = jnp.var(x, axis=axis, keepdims=True)
    return (x - m) / jnp.sqrt(v + eps)

def _scatter_add(tgt, idx, src, axis=0):
    return tgt.at[idx].add(src)

def _segment_sum(src, seg, n):
    return jax.ops.segment_sum(src, seg, n)
kernel_name = 'mk_conv_seq_d2_conv_nchw512_r4_beae93'

def setup_inputs(seed: int=0):
    np.random.seed(seed)
    _w = jnp.asarray

    def _rec_inputs():
        import jax
        import jax.numpy as jnp
        _gk = jax.random.key(seed)
        x = 7.22e-05 + 1 * jax.random.normal(jax.random.fold_in(_gk, 1), (16, 128, 32, 32), jnp.float32)
        return x
    x = _rec_inputs()

    def _L0_conv_setup():
        import jax, jax.numpy as jnp
        import numpy as np
        NUM_HEADS = 8
        NUM_GROUPS = 32
        EPS = 1e-05
        RESCALE = 1.0

        def _group_norm(x, w, b):
            B, C, L = x.shape
            g = x.reshape(B, NUM_GROUPS, C // NUM_GROUPS * L)
            mu = jnp.mean(g, axis=-1, keepdims=True)
            var = jnp.var(g, axis=-1, keepdims=True)
            g = (g - mu) * jax.lax.rsqrt(var + EPS)
            return g.reshape(B, C, L) * w[None, :, None] + b[None, :, None]
        key = jax.random.key(seed)
        ks = jax.random.split(key, 7)
        b, c, h, w = (16, 128, 32, 32)
        return {'x': jax.random.normal(ks[0], (b, c, h, w), jnp.float32), 'norm_w': jax.random.normal(ks[1], (c,), jnp.float32), 'norm_b': jax.random.normal(ks[2], (c,), jnp.float32), 'qkv_w': jax.random.normal(ks[3], (3 * c, c), jnp.float32) * c ** (-0.5), 'qkv_b': jax.random.normal(ks[4], (3 * c,), jnp.float32) * 0.02, 'proj_w': jax.random.normal(ks[5], (c, c), jnp.float32) * c ** (-0.5), 'proj_b': jax.random.normal(ks[6], (c,), jnp.float32) * 0.02}
    _L0_conv_all = _L0_conv_setup()
    _L0_conv_in = {k: v for k, v in _L0_conv_all.items() if k in ('norm_w', 'norm_b', 'qkv_w', 'qkv_b', 'proj_w', 'proj_b')}
    del _L0_conv_all

    def _L1_conv_setup():
        import jax, jax.numpy as jnp
        import numpy as np
        EPS = 1e-08

        def rmsnorm2d(x, weight):
            rms = jnp.mean(jnp.square(x), axis=1, keepdims=True)
            return x * jax.lax.rsqrt(rms + EPS) * weight

        def conv1x1(x, w, b):
            y = jnp.einsum('bchw,oc->bohw', x, w)
            return y + b[None, :, None, None]
        dim, exp = (128, 4)
        hidden = dim * exp
        key = jax.random.key(seed)
        ks = jax.random.split(key, 8)
        s = 1.0 / np.sqrt(dim)
        sh = 1.0 / np.sqrt(hidden)
        return {'x': jax.random.normal(ks[0], (16, dim, 16, 16), dtype=jnp.float32), 'norm1_w': jnp.ones((1, dim, 1, 1), dtype=jnp.float32), 'conv_w': jax.random.uniform(ks[1], (dim, dim), jnp.float32, -s, s), 'conv_b': jax.random.uniform(ks[2], (dim,), jnp.float32, -s, s), 'norm2_w': jnp.ones((1, dim, 1, 1), dtype=jnp.float32), 'ffn_w1': jax.random.uniform(ks[3], (hidden, dim), jnp.float32, -s, s), 'ffn_b1': jax.random.uniform(ks[4], (hidden,), jnp.float32, -s, s), 'ffn_w2': jax.random.uniform(ks[5], (dim, hidden), jnp.float32, -sh, sh), 'ffn_b2': jax.random.uniform(ks[6], (dim,), jnp.float32, -sh, sh)}
    _L1_conv_all = _L1_conv_setup()
    _L1_conv_in = {k: v for k, v in _L1_conv_all.items() if k in ('norm1_w', 'conv_w', 'conv_b', 'norm2_w', 'ffn_w1', 'ffn_b1', 'ffn_w2', 'ffn_b2')}
    del _L1_conv_all
    return {'x': x, 'L0_conv_norm_w': _L0_conv_in['norm_w'], 'L0_conv_norm_b': _L0_conv_in['norm_b'], 'L0_conv_qkv_w': _L0_conv_in['qkv_w'], 'L0_conv_qkv_b': _L0_conv_in['qkv_b'], 'L0_conv_proj_w': _L0_conv_in['proj_w'], 'L0_conv_proj_b': _L0_conv_in['proj_b'], 'L1_conv_norm1_w': _L1_conv_in['norm1_w'], 'L1_conv_conv_w': _L1_conv_in['conv_w'], 'L1_conv_conv_b': _L1_conv_in['conv_b'], 'L1_conv_norm2_w': _L1_conv_in['norm2_w'], 'L1_conv_ffn_w1': _L1_conv_in['ffn_w1'], 'L1_conv_ffn_b1': _L1_conv_in['ffn_b1'], 'L1_conv_ffn_w2': _L1_conv_in['ffn_w2'], 'L1_conv_ffn_b2': _L1_conv_in['ffn_b2']}

def reference(x, L0_conv_norm_w, L0_conv_norm_b, L0_conv_qkv_w, L0_conv_qkv_b, L0_conv_proj_w, L0_conv_proj_b, L1_conv_norm1_w, L1_conv_conv_w, L1_conv_conv_b, L1_conv_norm2_w, L1_conv_ffn_w1, L1_conv_ffn_b1, L1_conv_ffn_w2, L1_conv_ffn_b2):
    import jax
    import jax.numpy as jnp

    def _L0_conv_ref(x, norm_w, norm_b, qkv_w, qkv_b, proj_w, proj_b):
        import jax, jax.numpy as jnp
        import numpy as np
        NUM_HEADS = 8
        NUM_GROUPS = 32
        EPS = 1e-05
        RESCALE = 1.0

        def _group_norm(x, w, b):
            B, C, L = x.shape
            g = x.reshape(B, NUM_GROUPS, C // NUM_GROUPS * L)
            mu = jnp.mean(g, axis=-1, keepdims=True)
            var = jnp.var(g, axis=-1, keepdims=True)
            g = (g - mu) * jax.lax.rsqrt(var + EPS)
            return g.reshape(B, C, L) * w[None, :, None] + b[None, :, None]
        b, c, hh, ww = x.shape
        L = hh * ww
        H = NUM_HEADS
        ch = c // H
        xr = x.reshape(b, c, L)
        hid = _group_norm(xr, norm_w, norm_b)
        qkv = jnp.einsum('oc,bcl->bol', qkv_w, hid) + qkv_b[None, :, None]
        qkv = qkv.reshape(b, H, 3, ch, L)
        q, k, v = (qkv[:, :, 0], qkv[:, :, 1], qkv[:, :, 2])
        scale = 1.0 / ch ** 0.25
        weight = jnp.einsum('bhct,bhcs->bhts', q * scale, k * scale)
        weight = jax.nn.softmax(weight.astype(jnp.float32), axis=-1).astype(weight.dtype)
        a = jnp.einsum('bhts,bhcs->bhct', weight, v)
        h = a.reshape(b, c, L)
        h = jnp.einsum('oc,bcl->bol', proj_w, h) + proj_b[None, :, None]
        h = h.reshape(b, c, hh, ww)
        return (x + h) / RESCALE

    def _L1_conv_ref(x, norm1_w, conv_w, conv_b, norm2_w, ffn_w1, ffn_b1, ffn_w2, ffn_b2):
        import jax, jax.numpy as jnp
        import numpy as np
        EPS = 1e-08

        def rmsnorm2d(x, weight):
            rms = jnp.mean(jnp.square(x), axis=1, keepdims=True)
            return x * jax.lax.rsqrt(rms + EPS) * weight

        def conv1x1(x, w, b):
            y = jnp.einsum('bchw,oc->bohw', x, w)
            return y + b[None, :, None, None]
        gelu = lambda t: jax.nn.gelu(t, approximate=False)
        h = gelu(rmsnorm2d(x, norm1_w))
        x = x + conv1x1(h, conv_w, conv_b)
        h = rmsnorm2d(x, norm2_w)
        h = gelu(conv1x1(h, ffn_w1, ffn_b1))
        x = x + conv1x1(h, ffn_w2, ffn_b2)
        return x

    def _gn(v, G=32, eps=1e-05):
        B_, C_, H_, W_ = v.shape
        g = v.reshape(B_, G, C_ // G, H_, W_)
        m = jnp.mean(g, axis=(2, 3, 4), keepdims=True)
        s = jnp.var(g, axis=(2, 3, 4), keepdims=True)
        return ((g - m) / jnp.sqrt(s + eps)).reshape(v.shape)

    def _ln_c(v, eps=1e-06):
        m = jnp.mean(v, axis=1, keepdims=True)
        s = jnp.var(v, axis=1, keepdims=True)
        return (v - m) / jnp.sqrt(s + eps)

    def _ln_t(v, eps=1e-05):
        m = jnp.mean(v, axis=-1, keepdims=True)
        s = jnp.var(v, axis=-1, keepdims=True)
        return (v - m) / jnp.sqrt(s + eps)

    def _to_tokens(v):
        B_, C_, H_, W_ = v.shape
        return v.reshape(B_, C_, H_ * W_).transpose(0, 2, 1)

    def _from_tokens(t, like):
        B_, C_, H_, W_ = like.shape
        return t.transpose(0, 2, 1).reshape(B_, C_, H_, W_)
    x = _L0_conv_ref(x, L0_conv_norm_w, L0_conv_norm_b, L0_conv_qkv_w, L0_conv_qkv_b, L0_conv_proj_w, L0_conv_proj_b)
    x = _L1_conv_ref(x, L1_conv_norm1_w, L1_conv_conv_w, L1_conv_conv_b, L1_conv_norm2_w, L1_conv_ffn_w1, L1_conv_ffn_b1, L1_conv_ffn_w2, L1_conv_ffn_b2)
    return x

_drawn_inputs = setup_inputs


def setup_inputs(seed=0):
    import zlib

    import numpy as np

    out = dict(_drawn_inputs(seed))
    spreads = {'L1_conv_norm1_w': (1.0, 0.2), 'L1_conv_norm2_w': (1.0, 0.553)}
    factors = {'L0_conv_qkv_b': 4.004,
     'L0_conv_proj_b': 3.537,
     'L1_conv_ffn_b1': 4.39,
     'L1_conv_ffn_b2': 3.014}
    for name, (base, spread) in spreads.items():
        noise = np.random.default_rng([zlib.crc32(name.encode()), seed]).standard_normal(out[name].shape)
        drawn = base * np.exp(spread * noise) if base else spread * noise
        out[name] = jnp.asarray(drawn.astype(out[name].dtype))
    for name, factor in factors.items():
        out[name] = (out[name] * factor).astype(out[name].dtype)
    return out
```

```python
import concourse.bass as bass
from concourse import mybir
from contextlib import ExitStack

IMAGES, C, PIXELS = 16, 128, 1024
HEADS, GROUPS, HIDDEN = 8, 32, 512
CH = C // HEADS
HALF = 512
NT = PIXELS // HALF
NK = PIXELS // 128
UNIT_HEADS = 4
UNITS = IMAGES * HEADS // UNIT_HEADS
STEPS = NT * NK
RING = 4
SPLIT = 3 * CH
ROWS = SPLIT + 2
GN_EPS, RMS_EPS = 1e-5, 1e-8
STACK_DMAS, ROW_DMAS, HEAD_DMAS, WEIGHT_DMAS = 12, 8, 8, 8
SCALE = 1.0 / CH ** 0.5
HB = HIDDEN // 128
(NORM_W, NORM_B, Q_B, K_B, PROJ_B, RMS1_W, CONV_B, RMS2_W, FFN_B2, FFN_B1) = range(10)
PARAMS = FFN_B1 + HB


def at_least(eng, sem, value):
    if isinstance(value, int) and value <= 0:
        return
    eng.wait_ge(sem, value)


def settled(eng, sem, value):
    eng.wait_ge(sem, value)


def held(eng, value):
    if not is_number(value):
        eng.compute_val(value)
    return value


def is_number(v):
    return isinstance(v, int)


def is_first(b):
    return is_number(b) and b == 0


def has_image(b):
    return not is_number(b) or 0 <= b < IMAGES


def has_unit(u):
    return not is_number(u) or 0 <= u < UNITS


def one(b):
    return slice(b, b + 1) if is_number(b) else bass.ds(b, 1)


def attention_block(nc, x, params, d):
    fp32, fp32r = mybir.dt.float32, mybir.dt.float32r
    ALU, ACT, AX = mybir.AluOpType, mybir.ActivationFunctionType, mybir.AxisListType
    with ExitStack() as ctx:
        def sb(name, shape, dt=fp32):
            return ctx.enter_context(nc.sbuf_tensor(name, shape, dt))

        def sem(name):
            return ctx.enter_context(nc.semaphore(name))

        q_stack = sb("q_stack", [128, RING, 2, PIXELS], fp32r)
        k_stack = sb("k_stack", [128, RING, 2, PIXELS], fp32r)
        probs = sb("probs", [128, 4, 2, HALF])
        values = sb("values", [128, 2, NK, HEADS, 32])
        hid = sb("hid", [128, PIXELS])
        q_full, k_full = sb("q_full", [128, PIXELS]), sb("k_full", [128, PIXELS])
        q_high, q_low = sb("q_high", [128, PIXELS], fp32r), sb("q_low", [128, PIXELS], fp32r)
        k_high, k_low = sb("k_high", [128, PIXELS], fp32r), sb("k_low", [128, PIXELS], fp32r)
        raw = sb("raw", [128, PIXELS])
        attn = sb("attn", [128, PIXELS])
        inv_den = sb("inv_den", [128, PIXELS])
        den = sb("den", [128, PIXELS // CH])
        inv = sb("inv", [128, PIXELS // CH])
        wq, wk, wv = sb("wq", [128, C]), sb("wk", [128, C]), sb("wv", [128, C])
        wp = sb("wp", [128, C])
        v_bias = sb("v_bias", [128, C])
        group_mean, identity = sb("group_mean", [128, C]), sb("identity", [128, C])
        maxes = sb("maxes", [128, 32, 2])
        neg_max = sb("neg_max", [128, 32])
        row_high, row_low = sb("row_high", [32, 128], fp32r), sb("row_low", [32, 128], fp32r)
        stats = sb("stats", [128, 2, 6])
        mean_var = sb("mean_var", [128, 2])
        gn = sb("gn", [128, 10])
        g_mean, g_dev, g_mix, g_var, g_rstd, g_scale, g_tmp, g_shift, neg_half, settle = (
            gn[:, i:i + 1] for i in range(10))

        psum = ctx.enter_context(nc.psum_tensor("psum", [128, 8, HALF], fp32))
        acc, misc = psum[:, 6, :], psum[:, 7, :]

        weights_in, x_in = sem("weights_in"), [sem(f"x_in{n}") for n in range(4)]
        x_rest_in = sem("x_rest_in")
        setup_done = sem("setup_done")
        stack_in, rows_in = sem("stack_in"), sem("rows_in")
        heads_in, inv_out, inv_in = sem("heads_in"), sem("inv_out"), sem("inv_in")
        stats_ready, gn_stats, gn_mean, gn_mix, gn_group, gn_var = (
            sem("stats_ready"), sem("gn_stats"), sem("gn_mean"), sem("gn_mix"), sem("gn_group"), sem("gn_var"))
        gn_scaled = sem("gn_scaled")
        hid_ready, qk_ready, qk_full, split_done = (
            sem("hid_ready"), sem("qk_ready"), sem("qk_full"), sem("split_done"))
        v_ready, v_full = sem("v_ready"), sem("v_full")
        max_ready, max_taken, neg_max_ready, max_turned, rows_ready = (
            sem("max_ready"), sem("max_taken"), sem("neg_max_ready"), sem("max_turned"), sem("rows_ready"))
        scores_ready, probs_ready, pv_done, acc_taken = (
            sem("scores_ready"), sem("probs_ready"), sem("pv_done"), sem("acc_taken"))
        inv_ready, attn_ready, proj_ready, proj_taken = (
            sem("inv_ready"), sem("attn_ready"), sem("proj_ready"), sem("proj_taken"))
        row_high_ready = sem("row_high_ready")
        dve_step, pool_step = sem("dve_step"), sem("pool_step")

        def run(eng, slot):
            def image(b, parity):
                for half in range(2):
                    slot(b, parity, half)
            for b in range(-2, 2):
                image(b, b % 2)
            with eng.Fori(1, IMAGES // 2 - 1) as i:
                for parity in range(2):
                    image(i * 2 + parity, parity)
            for b in range(IMAGES - 2, IMAGES + 1):
                image(b, b % 2)

        def image_of_x(b, lo, n):
            return x[:, one(b), lo:lo + n].squeeze(1)

        block = ctx.enter_context(nc.Block())

        @block.sync
        def _(sp):
            def load_x(b, signal):
                sp.dma_start(x[:, b, :], d["x"][b]).then_inc(signal, 16)

            def stack(done, parity, half):
                sp.wait_ge(split_done, done)
                for j in range(2):
                    rows = slice(64 * half + 32 * j, 64 * half + 32 * j + 32)
                    for dst, parts in ((q_stack, (q_high, q_high, q_low)), (k_stack, (k_high, k_low, k_high))):
                        for n, part in enumerate(parts):
                            at = 64 * j + CH * n
                            sp.dma_start(dst[at:at + CH, 2 * parity + half, :, :].bitcast(fp32),
                                         part[rows, :].bitcast(fp32)).then_inc(stack_in, 16)

            def maximum_rows(parity, half):
                for p in range(2):
                    for j in range(2):
                        head = 2 * p + j
                        for n, src in enumerate((row_high, row_low)):
                            at = 64 * j + SPLIT + n
                            row = q_stack[at:at + 1, 2 * parity + half, p, :].bitcast(fp32)
                            sp.dma_start(row.rearrange("o (k f) -> o k f", f=128),
                                         src[NK * head:NK * head + NK, :].bitcast(fp32)).then_inc(rows_in, 16)

            def heads(half):
                for g in range(UNIT_HEADS):
                    h = UNIT_HEADS * half + g
                    rows = slice(CH * h, CH * h + CH)
                    sp.dma_start(attn[rows, :], raw[32 * g:32 * g + CH, :]).then_inc(heads_in, 16)
                    sp.dma_start(den[rows, :], raw[32 * g + CH:32 * g + CH + 1, :].rearrange(
                        "o (k f) -> o k f", k=CH)).then_inc(heads_in, 16)

            def slot(b, parity, half):
                u = b * 2 + half
                scored = held(sp, u * (2 * STEPS))
                taken, placed = held(sp, u * NT), held(sp, (u - 1) * (16 * HEAD_DMAS))
                turned, rowed = held(sp, u + 2), held(sp, (u + 1) * (16 * ROW_DMAS))
                if half == 0:
                    split, stacked = held(sp, (b + 2) * 2), held(sp, (b + 1) * (2 * 16 * STACK_DMAS) + 16 * STACK_DMAS)
                    inverted, written, projected = held(sp, b), held(sp, b * 16), held(sp, (b - 1) * NT)
                else:
                    split, stacked = held(sp, (b + 3) * 2), held(sp, (b + 2) * (2 * 16 * STACK_DMAS))
                    inverted, projected = held(sp, b + 0), held(sp, b * NT)
                if half == 0 and has_image(b + 1):
                    at_least(sp, scores_ready, scored)
                    at_least(sp, stack_in, stacked)
                    stack(split, 1 - parity, 1)
                if has_unit(u - 1):
                    at_least(sp, acc_taken, taken)
                    if half == 1:
                        at_least(sp, proj_ready, projected)
                        at_least(sp, inv_ready, inverted)
                    at_least(sp, heads_in, placed)
                    heads(1 - half)
                if has_unit(u + 1):
                    sp.wait_ge(rows_ready, turned)
                    at_least(sp, rows_in, rowed)
                    maximum_rows(parity if half == 0 else 1 - parity, 1 - half)
                if is_first(b) and half == 0:
                    for n in range(4, IMAGES):
                        load_x(n, x_rest_in)
                if half == 0 and has_image(b - 1):
                    sp.wait_ge(inv_ready, inverted)
                    at_least(sp, proj_ready, projected)
                    sp.dma_start(d["inv"].rearrange("h (k f) -> (h k) f", k=CH), inv[:, :]).then_inc(inv_out, 16)
                    sp.wait_ge(inv_out, written)
                    for h in range(HEADS):
                        sp.dma_start(inv_den[CH * h:CH * h + CH, :],
                                     d["inv"][h:h + 1, :].broadcast_to([CH, PIXELS])).then_inc(inv_in, 16)
                if half == 1 and has_image(b + 2):
                    at_least(sp, scores_ready, scored)
                    at_least(sp, stack_in, stacked)
                    stack(split, parity, 0)

            load_x(0, x_in[0])
            for tile, name in ((wq, "wq"), (wk, "wk"), (wv, "wv"), (wp, "wp"), (group_mean, "group_mean"),
                               (identity, "identity"), (params, "params")):
                sp.dma_start(tile[:, :], d[name]).then_inc(weights_in, 16)
            sp.dma_start(v_bias[:, :], d["v_bias"].broadcast_to([128, C])).then_inc(weights_in, 16)
            for n in range(1, 4):
                load_x(n, x_in[n])
            sp.wait_ge(setup_done, 3)
            run(sp, slot)

        @block.gpsimd
        def _(pool):
            steps = [0]

            def slot(b, parity, half):
                if half == 0 and has_image(b - 1):
                    pool.wait_ge(inv_in, b * (16 * HEADS))
                    pool.wait_ge(heads_in, b * (2 * 16 * HEAD_DMAS))
                    nc.gpsimd.tensor_tensor(out=attn[:, :], in0=attn[:, :], in1=inv_den[:, :],
                                            op=ALU.mult).then_inc(attn_ready, 1)
                if half == 0 and has_image(b + 2):
                    pool.wait_ge(gn_var, b + 3)
                    nc.gpsimd.tensor_tensor(out=g_rstd, in0=g_var, in1=neg_half, op=ALU.pow).then_inc(pool_step, 1)
                    pool.wait_ge(pool_step, b * 3 + 7)
                    nc.gpsimd.tensor_tensor(out=g_scale, in0=g_rstd, in1=params[:, NORM_W:NORM_W + 1],
                                            op=ALU.mult).then_inc(pool_step, 1)
                    pool.wait_ge(pool_step, b * 3 + 8)
                    nc.gpsimd.tensor_tensor(out=g_tmp, in0=g_mean, in1=g_scale, op=ALU.mult).then_inc(pool_step, 1)
                    pool.wait_ge(pool_step, b * 3 + 9)
                    nc.gpsimd.tensor_tensor(out=g_shift, in0=params[:, NORM_B:NORM_B + 1], in1=g_tmp,
                                            op=ALU.subtract).then_inc(gn_scaled, 1)
                if half == 1 and has_image(b + 2):
                    pool.wait_ge(qk_full, (b + 2) * 4 + 4)
                    nc.gpsimd.tensor_tensor(out=q_low[:, :], in0=q_full[:, :], in1=q_high[:, :].bitcast(fp32),
                                            op=ALU.subtract).then_inc(split_done, 1)
                    nc.gpsimd.tensor_tensor(out=k_low[:, :], in0=k_full[:, :], in1=k_high[:, :].bitcast(fp32),
                                            op=ALU.subtract).then_inc(split_done, 1)

            run(pool, slot)

        @block.tensor
        def _(pe):
            def values_of(c, part):
                if part == 0:
                    pe.wait_ge(hid_ready, c + 1)
                for k in range(4):
                    chunk = 4 * part + k
                    last = nc.tensor.matmul(misc[:, 128 * k:128 * k + 128], hid[:, 128 * chunk:128 * chunk + 128],
                                            wv[:, :], start=True, stop=True)
                last.then_inc(v_ready, 1)

            def side_jobs(b, parity, half, s):
                u = b * 2 + half
                c = b + 2
                if half == 0:
                    if s == 1 and has_unit(u + 1):
                        pe.wait_ge(neg_max_ready, u + 2)
                        at_least(pe, rows_ready, u + 1)
                        nc.tensor.transpose(misc[0:32, 0:128], neg_max[:, :], identity[:, :]).then_inc(max_turned, 1)
                    if s == 2 and has_image(c):
                        at_least(pe, rows_ready, u + 2)
                        if is_number(b):
                            at_least(pe, qk_full, (b + 2) * 4)
                        pe.wait_ge(gn_stats, b + 3)
                        nc.tensor.matmul(misc[:, 0:1], group_mean[:, :], mean_var[:, 0:1],
                                         start=True, stop=True).then_inc(gn_mean, 1)
                    if s == 4 and has_image(b + 1):
                        at_least(pe, rows_ready, u + 2)
                        if has_image(c):
                            pe.wait_ge(gn_mix, b + 3)
                        values_of(b + 1, 0)
                    if s == 6 and has_image(b + 1):
                        pe.wait_ge(v_full, b * 2 + 3)
                        values_of(b + 1, 1)
                    if s == 8 and has_image(c):
                        at_least(pe, v_full, b * 2 + 4)
                        pe.wait_ge(gn_mix, b + 3)
                        nc.tensor.matmul(misc[:, 0:1], group_mean[:, :], g_mix, start=True, stop=True).then_inc(gn_group, 1)
                    if s in (11, 13) and has_image(b - 1):
                        t = (s - 11) // 2
                        if t == 0:
                            if has_image(c):
                                pe.wait_ge(gn_var, b + 3)
                            else:
                                at_least(pe, v_full, min(b + 2, IMAGES) * 2)
                                at_least(pe, rows_ready, min(u + 2, UNITS))
                                at_least(pe, proj_taken, (b - 1) * 2)
                            pe.wait_ge(attn_ready, b)
                        else:
                            pe.wait_ge(proj_taken, b * 2 - 1)
                        nc.tensor.matmul(misc, wp[:, :], attn[:, HALF * t:HALF * t + HALF],
                                         start=True, stop=True).then_inc(proj_ready, 1)
                else:
                    if 1 <= s <= 4 and has_image(c):
                        if s == 1:
                            pe.wait_ge(hid_ready, b + 3)
                            at_least(pe, gn_var, b + 3)
                            at_least(pe, proj_taken, b * 2)
                        else:
                            pe.wait_ge(qk_full, b * 4 + 7 + s)
                        weight, t = ((wq, 0), (wq, 1), (wk, 0), (wk, 1))[s - 1]
                        nc.tensor.matmul(misc, weight[:, :], hid[:, HALF * t:HALF * t + HALF],
                                         start=True, stop=True).then_inc(qk_ready, 1)
                    if s == 6 and has_unit(u + 1):
                        if has_image(c):
                            pe.wait_ge(qk_full, b * 4 + 12)
                        else:
                            at_least(pe, proj_taken, b * 2)
                        pe.wait_ge(neg_max_ready, u + 2)
                        nc.tensor.transpose(misc[0:32, 0:128], neg_max[:, :], identity[:, :]).then_inc(max_turned, 1)

            def maximum_scores(u, place, s, k):
                j, key_half, p, chunk = k % 2, k // 2, s % 2, s // 2
                rows = slice(64 * j, 64 * j + SPLIT)
                if s == 0 and k == 0:
                    pe.wait_ge(stack_in, u * (16 * STACK_DMAS) + 16 * STACK_DMAS)
                at_least(pe, max_taken, u * (4 * STEPS) + (4 * s + k - 1))
                nc.tensor.matmul(psum[:, 4 + j, :], q_stack[rows, place, p, 128 * chunk:128 * chunk + 128],
                                 k_stack[rows, place, p, HALF * key_half:HALF * key_half + HALF],
                                 start=True, stop=True).then_inc(max_ready, 1)

            def scores(u, place, s, k):
                j, p, t, chunk = 1 - k % 2, k // 2, s // NK, s % NK
                rows = slice(64 * j, 64 * j + ROWS)
                if s == 0 and k == 0:
                    pe.wait_ge(rows_in, u * (16 * ROW_DMAS) + 16 * ROW_DMAS)
                if k % 2 == 0:
                    at_least(pe, probs_ready, u * (2 * STEPS) + (2 * s + p - 1))
                mm = nc.tensor.matmul(psum[:, 2 * p + j, :], k_stack[rows, place, p, 128 * chunk:128 * chunk + 128],
                                      q_stack[rows, place, p, HALF * t:HALF * t + HALF], start=True, stop=True)
                if k % 2 == 1:
                    mm.then_inc(scores_ready, 1)

            def weigh_values(u, parity, half, s):
                chunk = s % NK
                pe.wait_ge(probs_ready, u * (2 * STEPS) + 2 * s + 2)
                if chunk == 0:
                    at_least(pe, acc_taken, u * NT + s // NK)
                if s == 0 and half == 0:
                    pe.wait_ge(v_full, u + 2)
                for g in range(UNIT_HEADS):
                    last = nc.tensor.matmul(acc[32 * g:32 * g + 32, :],
                                            values[:, parity, chunk, UNIT_HEADS * half + g, :],
                                            probs[:, (2 * s + g // 2) % 4, g % 2, :],
                                            start=(chunk == 0), stop=(chunk == NK - 1))
                last.then_inc(pv_done, 1)

            def slot(b, parity, half):
                u = b * 2 + half
                for s in range(STEPS):
                    side_jobs(b, parity, half, s)
                    for k in range(4):
                        if has_unit(u + 2):
                            maximum_scores(u + 2, 2 * (1 - parity) + half, s, k)
                        if has_unit(u):
                            scores(u, 2 * parity + half, s, k)
                    if s == 0:
                        if has_unit(u - 1):
                            if half == 0:
                                weigh_values(u - 1, 1 - parity, 1, STEPS - 1)
                            else:
                                weigh_values(u - 1, parity, 0, STEPS - 1)
                    elif has_unit(u):
                        weigh_values(u, parity, half, s - 1)

            pe.wait_ge(weights_in, 16 * WEIGHT_DMAS)
            pe.wait_ge(setup_done, 3)
            run(pe, slot)

        @block.scalar
        def _(act):
            def slot(b, parity, half):
                u = b * 2 + half
                for s in range(STEPS):
                    if has_unit(u):
                        for p in range(2):
                            act.wait_ge(scores_ready, u * (2 * STEPS) + 2 * s + p + 1)
                            at_least(act, pv_done, u * STEPS + s - 1)
                            nc.scalar.activation(probs[:, (2 * s + p) % 4, :, :], psum[:, 2 * p:2 * p + 2, :],
                                                 ACT.Exp, scale=SCALE).then_inc(probs_ready, 1)
                    if s % NK == 0 and (has_unit(u) and s or has_unit(u - 1) and not s):
                        t = 0 if s else 1
                        v = u if s else u - 1
                        act.wait_ge(pv_done, v * STEPS + NK * (t + 1))
                        at_least(act, heads_in, v * (16 * HEAD_DMAS))
                        nc.scalar.copy(raw[:, HALF * t:HALF * t + HALF], acc).then_inc(acc_taken, 1)
                    if half == 1 and 1 <= s <= 4 and has_image(b + 2):
                        act.wait_ge(qk_ready, b * 4 + 8 + s)
                        if s == 1:
                            at_least(act, split_done, (b + 2) * 2)
                            at_least(act, stack_in, (b + 2) * (2 * 16 * STACK_DMAS))
                        t = (s - 1) % 2
                        full, high, bias = ((q_full, q_high, Q_B), (k_full, k_high, K_B))[(s - 1) // 2]
                        for out in (full, high):
                            last = nc.scalar.activation(out[:, HALF * t:HALF * t + HALF], misc, ACT.Identity,
                                                        bias=params[:, bias:bias + 1])
                        last.then_inc(qk_full, 1)

            act.wait_ge(weights_in, 16 * WEIGHT_DMAS)
            run(act, slot)

        @block.vector
        def _(dve):
            def take_maxima(u, s):
                for k in range(4):
                    j, key_half, p, chunk = k % 2, k // 2, s % 2, s // 2
                    dve.wait_ge(max_ready, u * (4 * STEPS) + 4 * s + k + 1)
                    if s == 0 and k == 0:
                        at_least(dve, neg_max_ready, u)
                    nc.vector.tensor_reduce(maxes[:, (2 * p + j) * NK + chunk, key_half:key_half + 1],
                                            psum[:, 4 + j, :], axis=AX.X, op=ALU.max).then_inc(max_taken, 1)

            def side_jobs(b, parity, half, s):
                u = b * 2 + half
                c = b + 2
                if s == (1 if half == 0 else 6) and has_unit(u + 1):
                    dve.wait_ge(max_turned, u + 2)
                    at_least(dve, rows_in, (u + 1) * (16 * ROW_DMAS))
                    nc.vector.tensor_copy(row_high[:, :], misc[0:32, 0:128]).then_inc(row_high_ready, 1)
                    dve.wait_ge(row_high_ready, u + 2)
                    nc.vector.tensor_tensor(out=row_low[:, :], in0=misc[0:32, 0:128], in1=row_high[:, :].bitcast(fp32),
                                            op=ALU.subtract).then_inc(rows_ready, 1)
                if half == 1:
                    return
                if s == 0 and has_image(c):
                    if is_number(c):
                        dve.wait_ge(x_in[c], 16)
                    else:
                        dve.wait_ge(x_rest_in, 16 * (IMAGES - 4))
                    for t in range(2):
                        nc.vector.bn_stats(stats[:, t, :], image_of_x(c, HALF * t, HALF)).then_inc(
                            stats_ready, 1)
                    dve.wait_ge(stats_ready, b * 2 + 6)
                    nc.vector.memset(settle, 0.0)
                    nc.vector.bn_aggr(mean_var[:, :], stats[:, :, :].rearrange("p a b -> p (a b)")).then_inc(gn_stats, 1)
                if s == 3 and has_image(c):
                    dve.wait_ge(gn_mean, b + 3)
                    at_least(dve, hid_ready, b + 2)
                    nc.vector.tensor_copy(g_mean, misc[:, 0:1]).then_inc(dve_step, 1)
                    dve.wait_ge(dve_step, b * 2 + 5)
                    nc.vector.tensor_tensor(out=g_dev, in0=mean_var[:, 0:1], in1=g_mean,
                                            op=ALU.subtract).then_inc(dve_step, 1)
                    dve.wait_ge(dve_step, b * 2 + 6)
                    nc.vector.scalar_tensor_tensor(out=g_mix, in0=g_dev, scalar=g_dev, in1=mean_var[:, 1:2],
                                                   op0=ALU.mult, op1=ALU.add).then_inc(gn_mix, 1)
                if s in (5, 7) and has_image(b + 1):
                    part = (s - 5) // 2
                    dve.wait_ge(v_ready, b * 2 + 3 + part)
                    at_least(dve, pv_done, u * STEPS)
                    for k in range(4):
                        last = nc.vector.tensor_tensor(
                            out=values[:, 1 - parity, 4 * part + k, :, 0:CH],
                            in0=misc[:, 128 * k:128 * k + 128].rearrange("p (h i) -> p h i", i=CH),
                            in1=v_bias[:, :].rearrange("p (h i) -> p h i", i=CH), op=ALU.add)
                    last.then_inc(v_full, 1)
                if s == 6 and has_image(b - 1):
                    dve.wait_ge(heads_in, b * (2 * 16 * HEAD_DMAS))
                    at_least(dve, inv_out, (b - 1) * 16)
                    nc.vector.reciprocal(inv[:, :], den[:, :]).then_inc(inv_ready, 1)
                if s == 9 and has_image(c):
                    dve.wait_ge(gn_group, b + 3)
                    nc.vector.tensor_scalar(g_var, misc[:, 0:1], GN_EPS, None, ALU.add).then_inc(gn_var, 1)
                if s == 11 and has_image(c):
                    dve.wait_ge(gn_scaled, b + 3)
                    at_least(dve, v_ready, (b + 2) * 2)
                    nc.vector.tensor_scalar(hid[:, :], image_of_x(c, 0, PIXELS), g_scale, g_shift,
                                            ALU.mult, ALU.add).then_inc(hid_ready, 1)
                if s in (12, 14) and has_image(b - 1):
                    t = (s - 12) // 2
                    dve.wait_ge(proj_ready, b * 2 - 1 + t)
                    nc.vector.scalar_tensor_tensor(
                        out=image_of_x(b - 1, HALF * t, HALF), in0=misc,
                        scalar=params[:, PROJ_B:PROJ_B + 1],
                        in1=image_of_x(b - 1, HALF * t, HALF),
                        op0=ALU.add, op1=ALU.add).then_inc(proj_taken, 1)

            def slot(b, parity, half):
                u = b * 2 + half
                for s in range(STEPS):
                    if has_unit(u + 2):
                        take_maxima(u + 2, s)
                    side_jobs(b, parity, half, s)
                if has_unit(u + 2):
                    dve.wait_ge(max_taken, (u + 3) * (4 * STEPS))
                    at_least(dve, max_turned, u + 2)
                    nc.vector.tensor_reduce(neg_max[:, :], maxes[:, :, :], axis=AX.X, op=ALU.max,
                                            negate=True).then_inc(neg_max_ready, 1)

            nc.vector.memset(k_stack[:, :, :, :].bitcast(fp32), 1.0).then_inc(setup_done, 1)
            nc.vector.memset(values[:, :, :, :, :], 1.0).then_inc(setup_done, 1)
            nc.vector.memset(neg_half, -0.5).then_inc(setup_done, 1)
            dve.wait_ge(weights_in, 16 * WEIGHT_DMAS)
            dve.wait_ge(setup_done, 3)
            run(dve, slot)


def ffn_block(nc, x, params, d):
    fp32 = mybir.dt.float32
    ALU, ACT = mybir.AluOpType, mybir.ActivationFunctionType
    with ExitStack() as ctx:
        def sb(name, shape, dt=fp32):
            return ctx.enter_context(nc.sbuf_tensor(name, shape, dt))

        def sem(name):
            return ctx.enter_context(nc.semaphore(name))

        wconv, w1, w2 = sb("wconv", [128, C]), sb("w1", [128, HIDDEN]), sb("w2", [128, HB, C])
        averager = sb("averager", [128, 32])
        square1, square2 = sb("square1", [128, PIXELS]), sb("square2", [128, PIXELS])
        sums = sb("sums", [128, HALF])
        rms_in, rms_out = sb("rms_in", [128, 16]), sb("rms_out", [128, 16])
        eps = sb("eps", [128, 16])
        mean_eps, neg_half = sb("mean_eps", [128, 16]), sb("neg_half2", [128, 16])
        inv_rms1, inv_rms2 = sb("inv_rms1", [128, PIXELS]), sb("inv_rms2", [128, PIXELS])
        normed1, act1 = sb("normed1", [128, PIXELS]), sb("act1", [128, PIXELS])
        normed2, act2 = sb("normed2", [128, PIXELS]), sb("act2", [128, NT, HB, HALF])
        result = sb("result", [128, PIXELS])
        psum = ctx.enter_context(nc.psum_tensor("psum2", [128, 8, HALF], fp32))

        weights_in, setup_done = sem("weights2_in"), sem("setup2_done")
        squares1, squares2, sums_ready, sums_taken = (
            sem("squares1"), sem("squares2"), sem("sums_ready"), sem("sums_taken"))
        rms_in_done, mean_ready, rms_ready, rms_stored, inv1_in, inv2_in = (
            sem("rms_in_done"), sem("mean_ready"), sem("rms_ready"), sem("rms_stored"), sem("inv1_in"), sem("inv2_in"))
        norm_step, normed1_ready, normed2_ready, act1_ready = (
            sem("norm_step"), sem("normed1_ready"), sem("normed2_ready"), sem("act1_ready"))
        conv_ready, conv_taken, hidden_ready, act2_ready, ffn_ready, result_ready, result_out = (
            sem("conv_ready"), sem("conv_taken"), sem("hidden_ready"), sem("act2_ready"), sem("ffn_ready"),
            sem("result_ready"), sem("result_out"))

        def run(eng, slot):
            for c in range(-2, 1):
                slot(c)
            with eng.Fori(1, IMAGES - 2) as c:
                slot(c)
            slot(IMAGES - 2)
            slot(IMAGES - 1)

        def image(b, lo=0, n=PIXELS):
            return x[:, one(b), lo:lo + n].squeeze(1)

        block = ctx.enter_context(nc.Block())

        @block.sync
        def _(sp):
            sp.dma_start(wconv[:, :], d["wconv"]).then_inc(weights_in, 16)
            sp.dma_start(w1[:, :], d["w1"]).then_inc(weights_in, 16)
            sp.dma_start(w2[:, :, :], d["w2"]).then_inc(weights_in, 16)

            def slot(c):
                made, stored = held(sp, c + 3), held(sp, c * 16 + 48)
                used2, used1, ended = held(sp, c + 1), held(sp, c + 2), held(sp, c * NT + NT)
                if norms(c):
                    sp.wait_ge(sums_taken, made)
                    for g in range(4):
                        sp.dma_start(rms_in[32 * g:32 * g + 32, :], sums[32 * g:32 * g + 1, :].rearrange(
                            "o (k f) -> o k f", k=32)).then_inc(rms_in_done, 16)
                    sp.wait_ge(rms_ready, made)
                    sp.dma_start(d["rms"].rearrange("a (k f) -> (a k) f", f=16), rms_out[:, :]).then_inc(rms_stored, 16)
                    sp.wait_ge(rms_stored, stored)
                    if has_image(c + 1):
                        at_least(sp, normed2_ready, used2)
                        sp.dma_start(inv_rms2[:, :], d["rms"][0:1, :].broadcast_to([128, PIXELS])).then_inc(inv2_in, 16)
                    if has_image(c + 2):
                        at_least(sp, normed1_ready, used1)
                        sp.dma_start(inv_rms1[:, :], d["rms"][1:2, :].broadcast_to([128, PIXELS])).then_inc(inv1_in, 16)
                if has_image(c):
                    sp.wait_ge(result_ready, ended)
                    settled(sp, weights_in, 48)
                    sp.dma_start(d["out"][one(c)].squeeze(0), result[:, :]).then_inc(result_out, 16)

            run(sp, slot)
            sp.wait_ge(result_out, 16 * IMAGES)

        @block.gpsimd
        def _(pool):
            nc.gpsimd.memset(neg_half[:, :], -0.5).then_inc(setup_done, 1)
            nc.gpsimd.memset(eps[:, :], RMS_EPS).then_inc(setup_done, 1)
            pool.wait_ge(setup_done, 3)

            def slot(c):
                if norms(c):
                    pool.wait_ge(rms_in_done, c * 64 + 192)
                    at_least(pool, rms_stored, c * 16 + 32)
                    nc.gpsimd.tensor_tensor(out=mean_eps[:, :], in0=rms_in[:, :], in1=eps[:, :],
                                            op=ALU.add).then_inc(mean_ready, 1)
                    pool.wait_ge(mean_ready, c + 3)
                    nc.gpsimd.tensor_tensor(out=rms_out[:, :], in0=mean_eps[:, :], in1=neg_half[:, :],
                                            op=ALU.pow).then_inc(rms_ready, 1)
            run(pool, slot)

        @block.tensor
        def _(pe):
            def convolve(c, t):
                if t == 0:
                    pe.wait_ge(act1_ready, c + 1)
                    at_least(pe, conv_taken, c * NT)
                else:
                    pe.wait_ge(conv_taken, c * NT + 1)
                nc.tensor.matmul(psum[:, 6, :], wconv[:, :], act1[:, HALF * t:HALF * t + HALF],
                                 start=True, stop=True).then_inc(conv_ready, 1)

            def hidden(c, t):
                for m in range(HB):
                    if t == 0 and m == 0:
                        pe.wait_ge(normed2_ready, c + 1)
                    at_least(pe, act2_ready, c * (NT * HB) + (t * HB + m - 3))
                    nc.tensor.matmul(psum[:, m, :], w1[:, 128 * m:128 * m + 128], normed2[:, HALF * t:HALF * t + HALF],
                                     start=True, stop=True).then_inc(hidden_ready, 1)

            def down(c, t):
                at_least(pe, result_ready, c * NT + (t - 1))
                for m in range(HB):
                    pe.wait_ge(act2_ready, c * (NT * HB) + (t * HB + m + 1))
                    mm = nc.tensor.matmul(psum[:, 4 + t, :], w2[:, m, :], act2[:, t, m, :],
                                          start=(m == 0), stop=(m == HB - 1))
                mm.then_inc(ffn_ready, 1)

            def sum_squares(c):
                at_least(pe, sums_taken, c + 2)
                sources = [(square2, squares2, c + 1), (square1, squares1, c + 2)]
                if not has_image(c + 1):
                    sources[0] = sources[1]
                if not has_image(c + 2):
                    sources[1] = sources[0]
                for g in range(4):
                    square, ready, b = sources[g // 2]
                    if g % 2 == 0:
                        pe.wait_ge(ready, b + 1)
                    t = g % 2
                    mm = nc.tensor.matmul(psum[32 * g:32 * g + 32, 7, :], averager[:, :],
                                          square[:, HALF * t:HALF * t + HALF], start=True, stop=True)
                mm.then_inc(sums_ready, 1)

            pe.wait_ge(weights_in, 48)
            pe.wait_ge(setup_done, 3)

            def slot(c):
                if has_image(c + 1):
                    convolve(c + 1, 0)
                if has_image(c):
                    hidden(c, 0)
                if has_image(c + 1):
                    convolve(c + 1, 1)
                if has_image(c):
                    down(c, 0)
                    hidden(c, 1)
                if norms(c):
                    sum_squares(c)
                if has_image(c):
                    down(c, 1)
            run(pe, slot)

        @block.scalar
        def _(act):
            def gelu_hidden(c, t):
                for m in range(HB):
                    act.wait_ge(hidden_ready, c * (NT * HB) + (t * HB + m + 1))
                    if m == 0:
                        at_least(act, ffn_ready, c * NT + (t - 1))
                    nc.scalar.activation(act2[:, t, m, :], psum[:, m, :], ACT.Gelu,
                                         bias=params[:, FFN_B1 + m:FFN_B1 + m + 1]).then_inc(act2_ready, 1)

            def slot(c):
                if has_image(c + 1):
                    act.wait_ge(normed1_ready, c + 2)
                    at_least(act, conv_ready, (c + 1) * NT)
                    nc.scalar.activation(act1[:, :], normed1[:, :], ACT.Gelu).then_inc(act1_ready, 1)
                if has_image(c + 2):
                    at_least(act, sums_ready, c + 2)
                    nc.scalar.activation(square1[:, :], image(c + 2), ACT.Square).then_inc(squares1, 1)
                if has_image(c):
                    gelu_hidden(c, 0)
                if has_image(c + 1):
                    act.wait_ge(conv_taken, (c + 1) * NT + NT)
                    at_least(act, sums_ready, c + 2)
                    nc.scalar.activation(square2[:, :], image(c + 1), ACT.Square).then_inc(squares2, 1)
                if has_image(c):
                    gelu_hidden(c, 1)
            run(act, slot)

        @block.vector
        def _(dve):
            nc.vector.memset(averager[:, :], 1.0 / C).then_inc(setup_done, 1)
            dve.wait_ge(weights_in, 48)

            def slot(c):
                if has_image(c + 1):
                    for t in range(NT):
                        dve.wait_ge(conv_ready, (c + 1) * NT + t + 1)
                        half = image(c + 1, HALF * t, HALF)
                        nc.vector.scalar_tensor_tensor(out=half, in0=psum[:, 6, :], scalar=params[:, CONV_B:CONV_B + 1],
                                                       in1=half, op0=ALU.add, op1=ALU.add).then_inc(conv_taken, 1)
                if has_image(c):
                    output_half(c, 0)
                if norms(c):
                    dve.wait_ge(sums_ready, c + 3)
                    at_least(dve, rms_in_done, c * 64 + 128)
                    nc.vector.tensor_copy(sums[:, :], psum[:, 7, :]).then_inc(sums_taken, 1)
                if has_image(c):
                    output_half(c, 1)
                if has_image(c + 1):
                    dve.wait_ge(inv2_in, (c + 2) * 16)
                    at_least(dve, hidden_ready, (c + 1) * (NT * HB))
                    nc.vector.scalar_tensor_tensor(out=normed2[:, :], in0=image(c + 1), scalar=params[:, RMS2_W:RMS2_W + 1],
                                                   in1=inv_rms2[:, :], op0=ALU.mult, op1=ALU.mult).then_inc(normed2_ready, 1)
                if has_image(c + 2):
                    dve.wait_ge(inv1_in, (c + 3) * 16)
                    at_least(dve, act1_ready, c + 2)
                    nc.vector.scalar_tensor_tensor(out=normed1[:, :], in0=image(c + 2), scalar=params[:, RMS1_W:RMS1_W + 1],
                                                   in1=inv_rms1[:, :], op0=ALU.mult, op1=ALU.mult).then_inc(normed1_ready, 1)

            def output_half(c, t):
                dve.wait_ge(ffn_ready, c * NT + t + 1)
                if t == 0:
                    at_least(dve, result_out, c * 16)
                nc.vector.scalar_tensor_tensor(out=result[:, HALF * t:HALF * t + HALF], in0=psum[:, 4 + t, :],
                                               scalar=params[:, FFN_B2:FFN_B2 + 1], in1=image(c, HALF * t, HALF),
                                               op0=ALU.add, op1=ALU.add).then_inc(result_ready, 1)
            run(dve, slot)


def norms(c):
    return has_image(c + 1) or has_image(c + 2)


def build(nc, d):
    fp32 = mybir.dt.float32
    with nc.sbuf_tensor("x_sb", [128, IMAGES, PIXELS], fp32) as x, nc.sbuf_tensor("params_sb", [128, PARAMS], fp32) as params:
        attention_block(nc, x, params, d)
        ffn_block(nc, x, params, d)


def kernel(x, L0_conv_norm_w, L0_conv_norm_b, L0_conv_qkv_w, L0_conv_qkv_b, L0_conv_proj_w, L0_conv_proj_b,
           L1_conv_norm1_w, L1_conv_conv_w, L1_conv_conv_b, L1_conv_norm2_w, L1_conv_ffn_w1, L1_conv_ffn_b1,
           L1_conv_ffn_w2, L1_conv_ffn_b2):
    import numpy as np
    import concourse.bacc as bacc
    from concourse.bass_utils import run_bass_kernel_spmd

    def flat(a):
        return np.asarray(a).reshape(-1)

    qkv_w = np.asarray(L0_conv_qkv_w).reshape(2, 2, 2, 3, CH, C)
    qkv_b = np.asarray(L0_conv_qkv_b).reshape(2, 2, 2, 3, CH)
    split_w = qkv_w.transpose(3, 5, 0, 2, 4, 1).reshape(3, C, C)
    split_b = qkv_b.transpose(3, 0, 2, 4, 1).reshape(3, C)
    value_w = qkv_w[:, :, :, 2].transpose(4, 0, 1, 2, 3).reshape(C, C)
    value_b = qkv_b[:, :, :, 2].reshape(1, C)
    group = np.arange(C) // (C // GROUPS)
    columns = [None] * PARAMS
    for at, v in ((NORM_W, L0_conv_norm_w), (NORM_B, L0_conv_norm_b), (Q_B, split_b[0]), (K_B, split_b[1]),
                  (PROJ_B, L0_conv_proj_b), (RMS1_W, L1_conv_norm1_w), (CONV_B, L1_conv_conv_b),
                  (RMS2_W, L1_conv_norm2_w), (FFN_B2, L1_conv_ffn_b2)):
        columns[at] = flat(v)
    for m in range(HB):
        columns[FFN_B1 + m] = flat(L1_conv_ffn_b1)[128 * m:128 * m + 128]
    arrays = {
        "x": np.asarray(x).reshape(IMAGES, C, PIXELS),
        "params": np.stack(columns, axis=1),
        "wq": split_w[0], "wk": split_w[1], "wv": value_w, "v_bias": value_b,
        "wp": np.asarray(L0_conv_proj_w).T,
        "group_mean": np.where(group[:, None] == group[None, :], np.float32(GROUPS / C), np.float32(0)).astype(np.float32),
        "identity": np.eye(C, dtype=np.float32),
        "wconv": np.asarray(L1_conv_conv_w).T,
        "w1": np.asarray(L1_conv_ffn_w1).T,
        "w2": np.asarray(L1_conv_ffn_w2).reshape(C, HB, 128).transpose(2, 1, 0),
    }
    arrays = {k: np.ascontiguousarray(v) for k, v in arrays.items()}
    nc = bacc.Bacc("TRN2", target_bir_lowering=False, num_devices=1)
    fp32 = mybir.dt.float32
    d = {k: nc.dram_tensor(f"in_{k}", v.shape, fp32, kind="ExternalInput").ap() for k, v in arrays.items()}
    d["out"] = nc.dram_tensor("out", (IMAGES, C, PIXELS), fp32, kind="ExternalOutput").ap()
    d["inv"] = nc.dram_tensor("inv_den_rows", (HEADS, PIXELS), fp32, kind="Internal").ap()
    d["rms"] = nc.dram_tensor("inv_rms_rows", (2, PIXELS), fp32, kind="Internal").ap()
    build(nc, d)
    r = run_bass_kernel_spmd(nc, [{f"in_{k}": v for k, v in arrays.items()}], core_ids=[0])
    return r.results[0]["out"].reshape(IMAGES, C, 32, 32)
```

```python
import concourse.bass as bass
from concourse import mybir
from contextlib import ExitStack

IMAGES, C, PIXELS = 16, 128, 1024
HEADS, GROUPS, HIDDEN = 8, 32, 512
CH = C // HEADS
HALF = 512
NT = PIXELS // HALF
NK = PIXELS // 128
UNIT_HEADS = 4
UNITS = IMAGES * HEADS // UNIT_HEADS
STEPS = NT * NK
RING = 4
SPLIT = 3 * CH
ROWS = 64
MAX_ROW = ROWS - 2
BANKS = 3
TILES = 4 * STEPS
GN_EPS, RMS_EPS = 1e-5, 1e-8
STACK_DMAS, ROW_DMAS, HEAD_DMAS, WEIGHT_DMAS = 12, 8, 8, 7
SCALE = 1.0 / CH ** 0.5
HB = HIDDEN // 128
CONV, FIRST = 2, 4
(NORM_W, NORM_B, Q_B, K_B, PROJ_B, RMS1_W, CONV_B, RMS2_W, FFN_B2, V_B, FFN_B1) = range(11)
PARAMS = FFN_B1 + HB


def at_least(eng, sem, value):
    if isinstance(value, int) and value <= 0:
        return
    eng.wait_ge(sem, value)


def settled(eng, sem, value):
    eng.wait_ge(sem, value)


def held(eng, value):
    if not is_number(value):
        eng.compute_val(value)
    return value


def is_number(v):
    return isinstance(v, int)


def score_head(k):
    return 2 * (k // 2) + 1 - k % 2


def is_first(b):
    return is_number(b) and b == 0


def has_image(b):
    return not is_number(b) or 0 <= b < IMAGES


def has_unit(u):
    return not is_number(u) or 0 <= u < UNITS


def one(b):
    return slice(b, b + 1) if is_number(b) else bass.ds(b, 1)


def attention_block(nc, x, params, d):
    fp32, fp32r = mybir.dt.float32, mybir.dt.float32r
    ALU, ACT, AX = mybir.AluOpType, mybir.ActivationFunctionType, mybir.AxisListType
    with ExitStack() as ctx:
        def sb(name, shape, dt=fp32):
            return ctx.enter_context(nc.sbuf_tensor(name, shape, dt))

        def sem(name):
            return ctx.enter_context(nc.semaphore(name))

        q_stack = sb("q_stack", [128, RING, 2, PIXELS], fp32r)
        k_stack = sb("k_stack", [128, RING, 2, PIXELS], fp32r)
        probs = sb("probs", [128, 8, HALF])
        values = sb("values", [128, 2, NK, HEADS, 32])
        hid = sb("hid", [128, PIXELS])
        q_full, k_full = sb("q_full", [128, PIXELS]), sb("k_full", [128, PIXELS])
        q_high, q_low = sb("q_high", [128, PIXELS], fp32r), sb("q_low", [128, PIXELS], fp32r)
        k_high, k_low = sb("k_high", [128, PIXELS], fp32r), sb("k_low", [128, PIXELS], fp32r)
        raw = sb("raw", [128, PIXELS])
        attn = sb("attn", [128, PIXELS])
        inv_den = sb("inv_den", [128, PIXELS])
        den = sb("den", [128, PIXELS // CH])
        inv = sb("inv", [128, PIXELS // CH])
        wq, wk, wv = sb("wq", [128, C]), sb("wk", [128, C]), sb("wv", [128, C])
        wp = sb("wp", [128, C])
        out_bias = sb("out_bias", [128, 1])
        group_mean, identity = sb("group_mean", [128, C]), sb("identity", [128, C])
        maxes = sb("maxes", [128, 32, 2])
        neg_max = sb("neg_max", [128, 32])
        row_high, row_low = sb("row_high", [32, 128], fp32r), sb("row_low", [32, 128], fp32r)
        stats = sb("stats", [128, 2, 6])
        mean_var = sb("mean_var", [128, 2])
        gn = sb("gn", [128, 10])
        g_mean, g_dev, g_mix, g_var, g_rstd, g_scale, g_tmp, g_shift, neg_half, settle = (
            gn[:, i:i + 1] for i in range(10))

        psum = ctx.enter_context(nc.psum_tensor("psum", [128, 8, HALF], fp32))
        acc, misc = psum[:, 6, :], psum[:, 7, :]

        weights_in, x_in = sem("weights_in"), [sem(f"x_in{n}") for n in range(4)]
        x_rest_in = sem("x_rest_in")
        setup_done = sem("setup_done")
        stack_in, rows_in = sem("stack_in"), sem("rows_in")
        heads_in, inv_out, inv_in = sem("heads_in"), sem("inv_out"), sem("inv_in")
        stats_ready, gn_stats, gn_mean, gn_mix, gn_group, gn_var = (
            sem("stats_ready"), sem("gn_stats"), sem("gn_mean"), sem("gn_mix"), sem("gn_group"), sem("gn_var"))
        gn_scaled = sem("gn_scaled")
        hid_ready, qk_ready, qk_full, split_done = (
            sem("hid_ready"), sem("qk_ready"), sem("qk_full"), sem("split_done"))
        v_ready, v_full = sem("v_ready"), sem("v_full")
        max_ready, max_taken, neg_max_ready, max_turned, rows_ready = (
            sem("max_ready"), sem("max_taken"), sem("neg_max_ready"), sem("max_turned"), sem("rows_ready"))
        scores_ready, probs_ready, pv_done, acc_taken = (
            sem("scores_ready"), sem("probs_ready"), sem("pv_done"), sem("acc_taken"))
        inv_ready, attn_ready, proj_ready, proj_taken = (
            sem("inv_ready"), sem("attn_ready"), sem("proj_ready"), sem("proj_taken"))
        row_high_ready = sem("row_high_ready")
        bias_ready, bias_taken = sem("bias_ready"), sem("bias_taken")
        dve_step, pool_step = sem("dve_step"), sem("pool_step")

        def run(eng, slot):
            def image(b, parity):
                for half in range(2):
                    slot(b, parity, half)
            for b in range(-2, 2):
                image(b, b % 2)
            with eng.Fori(1, IMAGES // 2 - 1) as i:
                for parity in range(2):
                    image(i * 2 + parity, parity)
            for b in range(IMAGES - 2, IMAGES + 1):
                image(b, b % 2)

        def image_of_x(b, lo, n):
            return x[:, one(b), lo:lo + n].squeeze(1)

        block = ctx.enter_context(nc.Block())

        @block.sync
        def _(sp):
            def load_x(b, signal):
                sp.dma_start(x[:, b, :], d["x"][b]).then_inc(signal, 16)

            def stack(done, parity, half):
                sp.wait_ge(split_done, done)
                for j in range(2):
                    rows = slice(64 * half + 32 * j, 64 * half + 32 * j + 32)
                    for dst, parts in ((q_stack, (q_high, q_high, q_low)), (k_stack, (k_high, k_low, k_high))):
                        for n, part in enumerate(parts):
                            at = 64 * j + CH * n
                            sp.dma_start(dst[at:at + CH, 2 * parity + half, :, :].bitcast(fp32),
                                         part[rows, :].bitcast(fp32)).then_inc(stack_in, 16)

            def maximum_rows(parity, half):
                for p in range(2):
                    for j in range(2):
                        head = 2 * p + j
                        for n, src in enumerate((row_high, row_low)):
                            at = ROWS * j + MAX_ROW + n
                            row = q_stack[at:at + 1, 2 * parity + half, p, :].bitcast(fp32)
                            sp.dma_start(row.rearrange("o (k f) -> o k f", f=128),
                                         src[NK * head:NK * head + NK, :].bitcast(fp32)).then_inc(rows_in, 16)

            def heads(half):
                for g in range(UNIT_HEADS):
                    h = UNIT_HEADS * half + g
                    rows = slice(CH * h, CH * h + CH)
                    sp.dma_start(attn[rows, :], raw[32 * g:32 * g + CH, :]).then_inc(heads_in, 16)
                    sp.dma_start(den[rows, :], raw[32 * g + CH:32 * g + CH + 1, :].rearrange(
                        "o (k f) -> o k f", k=CH)).then_inc(heads_in, 16)

            def slot(b, parity, half):
                u = b * 2 + half
                scored = held(sp, u * TILES)
                taken, placed = held(sp, u * NT), held(sp, (u - 1) * (16 * HEAD_DMAS))
                turned, rowed = held(sp, u + 2), held(sp, (u + 1) * (16 * ROW_DMAS))
                if half == 0:
                    split, stacked = held(sp, (b + 2) * 2), held(sp, (b + 1) * (2 * 16 * STACK_DMAS) + 16 * STACK_DMAS)
                    inverted, written, projected = held(sp, b), held(sp, b * 16), held(sp, (b - 1) * NT)
                else:
                    split, stacked = held(sp, (b + 3) * 2), held(sp, (b + 2) * (2 * 16 * STACK_DMAS))
                    inverted, projected = held(sp, b + 0), held(sp, b * NT)
                if half == 0 and has_image(b + 1):
                    at_least(sp, scores_ready, scored)
                    at_least(sp, stack_in, stacked)
                    stack(split, 1 - parity, 1)
                if has_unit(u - 1):
                    at_least(sp, acc_taken, taken)
                    if half == 1:
                        at_least(sp, proj_ready, projected)
                        at_least(sp, inv_ready, inverted)
                    at_least(sp, heads_in, placed)
                    heads(1 - half)
                if has_unit(u + 1):
                    sp.wait_ge(rows_ready, turned)
                    at_least(sp, rows_in, rowed)
                    maximum_rows(parity if half == 0 else 1 - parity, 1 - half)
                if is_first(b) and half == 0:
                    for n in range(4, IMAGES):
                        load_x(n, x_rest_in)
                if half == 0 and has_image(b - 1):
                    sp.wait_ge(inv_ready, inverted)
                    at_least(sp, proj_ready, projected)
                    sp.dma_start(d["inv"].rearrange("h (k f) -> (h k) f", k=CH), inv[:, :]).then_inc(inv_out, 16)
                    sp.wait_ge(inv_out, written)
                    for h in range(HEADS):
                        sp.dma_start(inv_den[CH * h:CH * h + CH, :],
                                     d["inv"][h:h + 1, :].broadcast_to([CH, PIXELS])).then_inc(inv_in, 16)
                if half == 1 and has_image(b + 2):
                    at_least(sp, scores_ready, scored)
                    at_least(sp, stack_in, stacked)
                    stack(split, parity, 0)

            load_x(0, x_in[0])
            for tile, name in ((wq, "wq"), (wk, "wk"), (wv, "wv"), (wp, "wp"), (group_mean, "group_mean"),
                               (identity, "identity"), (params, "params")):
                sp.dma_start(tile[:, :], d[name]).then_inc(weights_in, 16)
            for n in range(1, 4):
                load_x(n, x_in[n])
            sp.wait_ge(setup_done, 4)
            run(sp, slot)

        @block.gpsimd
        def _(pool):
            def slot(b, parity, half):
                if half == 0 and has_image(b - 1):
                    pool.wait_ge(inv_in, b * (16 * HEADS))
                    pool.wait_ge(heads_in, b * (2 * 16 * HEAD_DMAS))
                    nc.gpsimd.tensor_tensor(out=attn[:, :], in0=attn[:, :], in1=inv_den[:, :],
                                            op=ALU.mult).then_inc(attn_ready, 1)
                if half == 0 and has_image(b + 2):
                    pool.wait_ge(gn_var, b + 3)
                    at_least(pool, hid_ready, b + 2)
                    nc.gpsimd.tensor_tensor(out=g_rstd, in0=g_var, in1=neg_half, op=ALU.pow).then_inc(pool_step, 1)
                    pool.wait_ge(pool_step, b * 3 + 7)
                    nc.gpsimd.tensor_tensor(out=g_scale, in0=g_rstd, in1=params[:, NORM_W:NORM_W + 1],
                                            op=ALU.mult).then_inc(pool_step, 1)
                    pool.wait_ge(pool_step, b * 3 + 8)
                    nc.gpsimd.tensor_tensor(out=g_tmp, in0=g_mean, in1=g_scale, op=ALU.mult).then_inc(pool_step, 1)
                    pool.wait_ge(pool_step, b * 3 + 9)
                    nc.gpsimd.tensor_tensor(out=g_shift, in0=params[:, NORM_B:NORM_B + 1], in1=g_tmp,
                                            op=ALU.subtract).then_inc(gn_scaled, 1)
                if half == 1 and has_image(b + 2):
                    pool.wait_ge(qk_full, (b + 2) * 4 + 4)
                    nc.gpsimd.tensor_tensor(out=q_low[:, :], in0=q_full[:, :], in1=q_high[:, :].bitcast(fp32),
                                            op=ALU.subtract).then_inc(split_done, 1)
                    nc.gpsimd.tensor_tensor(out=k_low[:, :], in0=k_full[:, :], in1=k_high[:, :].bitcast(fp32),
                                            op=ALU.subtract).then_inc(split_done, 1)

            nc.gpsimd.memset(q_stack[:, :, :, :].bitcast(fp32), 0.0).then_inc(setup_done, 1)
            pool.wait_ge(weights_in, 16 * WEIGHT_DMAS)
            run(pool, slot)

        @block.tensor
        def _(pe):
            def values_of(c, part):
                if part == 0:
                    pe.wait_ge(hid_ready, c + 1)
                for k in range(4):
                    chunk = 4 * part + k
                    last = nc.tensor.matmul(misc[:, 128 * k:128 * k + 128], hid[:, 128 * chunk:128 * chunk + 128],
                                            wv[:, :], start=True, stop=True)
                last.then_inc(v_ready, 1)

            def side_jobs(b, parity, half, s):
                u = b * 2 + half
                c = b + 2
                if half == 0:
                    if s == 1 and has_unit(u + 1):
                        pe.wait_ge(neg_max_ready, u + 2)
                        at_least(pe, rows_ready, u + 1)
                        nc.tensor.transpose(misc[0:32, 0:128], neg_max[:, :], identity[:, :]).then_inc(max_turned, 1)
                    if s == 2 and has_image(c):
                        at_least(pe, rows_ready, u + 2)
                        if is_number(b):
                            at_least(pe, qk_full, (b + 2) * 4)
                        pe.wait_ge(gn_stats, b + 3)
                        nc.tensor.matmul(misc[:, 0:1], group_mean[:, :], mean_var[:, 0:1],
                                         start=True, stop=True).then_inc(gn_mean, 1)
                    if s == 4 and has_image(b + 1):
                        at_least(pe, rows_ready, u + 2)
                        if has_image(c):
                            pe.wait_ge(gn_mix, b + 3)
                        values_of(b + 1, 0)
                    if s == 6 and has_image(b + 1):
                        pe.wait_ge(v_full, b * 2 + 3)
                        values_of(b + 1, 1)
                    if s == 8 and has_image(c):
                        at_least(pe, v_full, b * 2 + 4)
                        pe.wait_ge(gn_mix, b + 3)
                        nc.tensor.matmul(misc[:, 0:1], group_mean[:, :], g_mix, start=True, stop=True).then_inc(gn_group, 1)
                    if s in (11, 13) and has_image(b - 1):
                        t = (s - 11) // 2
                        if t == 0:
                            if has_image(c):
                                pe.wait_ge(gn_var, b + 3)
                            else:
                                at_least(pe, v_full, min(b + 2, IMAGES) * 2)
                                at_least(pe, rows_ready, min(u + 2, UNITS))
                                at_least(pe, proj_taken, (b - 1) * 2)
                            pe.wait_ge(attn_ready, b)
                        else:
                            pe.wait_ge(proj_taken, b * 2 - 1)
                        nc.tensor.matmul(misc, wp[:, :], attn[:, HALF * t:HALF * t + HALF],
                                         start=True, stop=True).then_inc(proj_ready, 1)
                else:
                    if 1 <= s <= 4 and has_image(c):
                        if s == 1:
                            pe.wait_ge(hid_ready, b + 3)
                            at_least(pe, gn_var, b + 3)
                            at_least(pe, proj_taken, b * 2)
                        else:
                            pe.wait_ge(qk_full, b * 4 + 7 + s)
                        weight, t = ((wq, 0), (wq, 1), (wk, 0), (wk, 1))[s - 1]
                        nc.tensor.matmul(misc, weight[:, :], hid[:, HALF * t:HALF * t + HALF],
                                         start=True, stop=True).then_inc(qk_ready, 1)
                    if s == 6 and has_unit(u + 1):
                        if has_image(c):
                            pe.wait_ge(qk_full, b * 4 + 12)
                        else:
                            at_least(pe, proj_taken, b * 2)
                        pe.wait_ge(neg_max_ready, u + 2)
                        nc.tensor.transpose(misc[0:32, 0:128], neg_max[:, :], identity[:, :]).then_inc(max_turned, 1)

            def wait_for_bank(u, tile, freed):
                if tile == 0:
                    at_least(pe, freed, u * TILES)
                elif tile >= BANKS:
                    at_least(pe, freed, u * TILES + (tile - BANKS + 1))

            def maximum_scores(u, place, s, k):
                j, key_half, p, chunk, tile = k % 2, k // 2, s % 2, s // 2, 4 * s + k
                rows = slice(ROWS * j, ROWS * j + MAX_ROW)
                if tile == 0:
                    pe.wait_ge(stack_in, u * (16 * STACK_DMAS) + 16 * STACK_DMAS)
                wait_for_bank(u, tile, max_taken)
                nc.tensor.matmul(psum[:, BANKS + tile % BANKS, :], q_stack[rows, place, p, 128 * chunk:128 * chunk + 128],
                                 k_stack[rows, place, p, HALF * key_half:HALF * key_half + HALF],
                                 start=True, stop=True).then_inc(max_ready, 1)

            def scores(u, place, s, k):
                head, t, chunk, tile = score_head(k), s // NK, s % NK, 4 * s + k
                rows = slice(ROWS * (head % 2), ROWS * (head % 2) + ROWS)
                p = head // 2
                if tile == 0:
                    pe.wait_ge(rows_in, u * (16 * ROW_DMAS) + 16 * ROW_DMAS)
                wait_for_bank(u, tile, probs_ready)
                nc.tensor.matmul(psum[:, tile % BANKS, :], k_stack[rows, place, p, 128 * chunk:128 * chunk + 128],
                                 q_stack[rows, place, p, HALF * t:HALF * t + HALF],
                                 start=True, stop=True).then_inc(scores_ready, 1)

            def weigh_values(u, parity, half, s):
                chunk = s % NK
                pe.wait_ge(probs_ready, u * TILES + (4 * s + 4))
                if chunk == 0:
                    at_least(pe, acc_taken, u * NT + s // NK)
                if s == 0 and half == 0:
                    pe.wait_ge(v_full, u + 2)
                for k in range(UNIT_HEADS):
                    g = score_head(k)
                    last = nc.tensor.matmul(acc[32 * g:32 * g + 32, :],
                                            values[:, parity, chunk, UNIT_HEADS * half + g, :],
                                            probs[:, (4 * s + k) % 8, :],
                                            start=(chunk == 0), stop=(chunk == NK - 1))
                last.then_inc(pv_done, 1)

            def slot(b, parity, half):
                u = b * 2 + half
                for s in range(STEPS):
                    side_jobs(b, parity, half, s)
                    for k in range(4):
                        if has_unit(u + 2):
                            maximum_scores(u + 2, 2 * (1 - parity) + half, s, k)
                        if has_unit(u):
                            scores(u, 2 * parity + half, s, k)
                    if s == 0:
                        if has_unit(u - 1):
                            if half == 0:
                                weigh_values(u - 1, 1 - parity, 1, STEPS - 1)
                            else:
                                weigh_values(u - 1, parity, 0, STEPS - 1)
                    elif has_unit(u):
                        weigh_values(u, parity, half, s - 1)

            pe.wait_ge(weights_in, 16 * WEIGHT_DMAS)
            pe.wait_ge(setup_done, 4)
            nc.tensor.matmul(misc[:, 0:1], wp[:, :], params[:, V_B:V_B + 1], start=True, stop=True).then_inc(bias_ready, 1)
            pe.wait_ge(bias_taken, 1)
            run(pe, slot)

        @block.scalar
        def _(act):
            def slot(b, parity, half):
                u = b * 2 + half
                for s in range(STEPS):
                    if has_unit(u):
                        for k in range(UNIT_HEADS):
                            tile = 4 * s + k
                            act.wait_ge(scores_ready, u * TILES + (tile + 1))
                            if k == 0:
                                at_least(act, pv_done, u * STEPS + (s - 1))
                            nc.scalar.activation(probs[:, tile % 8, :], psum[:, tile % BANKS, :],
                                                 ACT.Exp, scale=SCALE).then_inc(probs_ready, 1)
                    if s % NK == 0 and (has_unit(u) and s or has_unit(u - 1) and not s):
                        t = 0 if s else 1
                        v = u if s else u - 1
                        act.wait_ge(pv_done, v * STEPS + NK * (t + 1))
                        at_least(act, heads_in, v * (16 * HEAD_DMAS))
                        nc.scalar.copy(raw[:, HALF * t:HALF * t + HALF], acc).then_inc(acc_taken, 1)
                    if half == 0 and s in (5, 7) and has_image(b + 1):
                        part = (s - 5) // 2
                        act.wait_ge(v_ready, b * 2 + 3 + part)
                        at_least(act, pv_done, u * STEPS)
                        nc.scalar.copy(values[:, 1 - parity, 4 * part:4 * part + 4, :, 0:CH],
                                       misc.rearrange("p (k h i) -> p k h i", k=4, i=CH)).then_inc(v_full, 1)
                    if half == 0 and s == 12 and has_image(b + 2):
                        act.wait_ge(gn_scaled, b + 3)
                        at_least(act, v_ready, (b + 2) * 2)
                        nc.scalar.activation(hid[:, :], image_of_x(b + 2, 0, PIXELS), ACT.Identity,
                                             bias=g_shift, scale=g_scale).then_inc(hid_ready, 1)
                    if half == 1 and 1 <= s <= 4 and has_image(b + 2):
                        act.wait_ge(qk_ready, b * 4 + 8 + s)
                        if s == 1:
                            at_least(act, split_done, (b + 2) * 2)
                            at_least(act, stack_in, (b + 2) * (2 * 16 * STACK_DMAS))
                        t = (s - 1) % 2
                        full, high, bias = ((q_full, q_high, Q_B), (k_full, k_high, K_B))[(s - 1) // 2]
                        for out in (full, high):
                            last = nc.scalar.activation(out[:, HALF * t:HALF * t + HALF], misc, ACT.Identity,
                                                        bias=params[:, bias:bias + 1])
                        last.then_inc(qk_full, 1)

            act.wait_ge(weights_in, 16 * WEIGHT_DMAS)
            act.wait_ge(setup_done, 4)
            run(act, slot)

        @block.vector
        def _(dve):
            def take_maxima(u, s):
                for k in range(4):
                    j, key_half, p, chunk = k % 2, k // 2, s % 2, s // 2
                    dve.wait_ge(max_ready, u * TILES + (4 * s + k + 1))
                    if s == 0 and k == 0:
                        at_least(dve, neg_max_ready, u)
                    nc.vector.tensor_reduce(maxes[:, (2 * p + j) * NK + chunk, key_half:key_half + 1],
                                            psum[:, BANKS + (4 * s + k) % BANKS, :], axis=AX.X, op=ALU.max).then_inc(max_taken, 1)

            def side_jobs(b, parity, half, s):
                u = b * 2 + half
                c = b + 2
                if s == (1 if half == 0 else 6) and has_unit(u + 1):
                    dve.wait_ge(max_turned, u + 2)
                    at_least(dve, rows_in, (u + 1) * (16 * ROW_DMAS))
                    nc.vector.tensor_copy(row_high[:, :], misc[0:32, 0:128]).then_inc(row_high_ready, 1)
                    dve.wait_ge(row_high_ready, u + 2)
                    nc.vector.tensor_tensor(out=row_low[:, :], in0=misc[0:32, 0:128], in1=row_high[:, :].bitcast(fp32),
                                            op=ALU.subtract).then_inc(rows_ready, 1)
                if half == 1:
                    return
                if s == 0 and has_image(c):
                    if is_number(c):
                        dve.wait_ge(x_in[c], 16)
                    else:
                        dve.wait_ge(x_rest_in, 16 * (IMAGES - 4))
                    for t in range(2):
                        nc.vector.bn_stats(stats[:, t, :], image_of_x(c, HALF * t, HALF)).then_inc(
                            stats_ready, 1)
                    dve.wait_ge(stats_ready, b * 2 + 6)
                    nc.vector.memset(settle, 0.0)
                    nc.vector.bn_aggr(mean_var[:, :], stats[:, :, :].rearrange("p a b -> p (a b)")).then_inc(gn_stats, 1)
                if s == 3 and has_image(c):
                    dve.wait_ge(gn_mean, b + 3)
                    at_least(dve, gn_scaled, b + 2)
                    nc.vector.tensor_copy(g_mean, misc[:, 0:1]).then_inc(dve_step, 1)
                    dve.wait_ge(dve_step, b * 2 + 5)
                    nc.vector.tensor_tensor(out=g_dev, in0=mean_var[:, 0:1], in1=g_mean,
                                            op=ALU.subtract).then_inc(dve_step, 1)
                    dve.wait_ge(dve_step, b * 2 + 6)
                    nc.vector.scalar_tensor_tensor(out=g_mix, in0=g_dev, scalar=g_dev, in1=mean_var[:, 1:2],
                                                   op0=ALU.mult, op1=ALU.add).then_inc(gn_mix, 1)
                if s == 6 and has_image(b - 1):
                    dve.wait_ge(heads_in, b * (2 * 16 * HEAD_DMAS))
                    at_least(dve, inv_out, (b - 1) * 16)
                    nc.vector.reciprocal(inv[:, :], den[:, :]).then_inc(inv_ready, 1)
                if s == 9 and has_image(c):
                    dve.wait_ge(gn_group, b + 3)
                    nc.vector.tensor_scalar(g_var, misc[:, 0:1], GN_EPS, None, ALU.add).then_inc(gn_var, 1)
                if s in (12, 14) and has_image(b - 1):
                    t = (s - 12) // 2
                    dve.wait_ge(proj_ready, b * 2 - 1 + t)
                    nc.vector.scalar_tensor_tensor(
                        out=image_of_x(b - 1, HALF * t, HALF), in0=misc,
                        scalar=out_bias[:, :],
                        in1=image_of_x(b - 1, HALF * t, HALF),
                        op0=ALU.add, op1=ALU.add).then_inc(proj_taken, 1)

            def slot(b, parity, half):
                u = b * 2 + half
                for s in range(STEPS):
                    if has_unit(u + 2):
                        take_maxima(u + 2, s)
                    side_jobs(b, parity, half, s)
                if has_unit(u + 2):
                    dve.wait_ge(max_taken, (u + 3) * TILES)
                    at_least(dve, max_turned, u + 2)
                    nc.vector.tensor_reduce(neg_max[:, :], maxes[:, :, :], axis=AX.X, op=ALU.max,
                                            negate=True).then_inc(neg_max_ready, 1)

            nc.vector.memset(k_stack[:, :, :, :].bitcast(fp32), 1.0).then_inc(setup_done, 1)
            nc.vector.memset(values[:, :, :, :, :], 1.0).then_inc(setup_done, 1)
            nc.vector.memset(neg_half, -0.5).then_inc(setup_done, 1)
            dve.wait_ge(weights_in, 16 * WEIGHT_DMAS)
            dve.wait_ge(setup_done, 4)
            dve.wait_ge(bias_ready, 1)
            nc.vector.tensor_tensor(out=out_bias[:, :], in0=misc[:, 0:1], in1=params[:, PROJ_B:PROJ_B + 1],
                                    op=ALU.add).then_inc(bias_taken, 1)
            dve.wait_ge(bias_taken, 1)
            run(dve, slot)


def ffn_block(nc, x, params, d):
    fp32 = mybir.dt.float32
    ALU, ACT = mybir.AluOpType, mybir.ActivationFunctionType
    with ExitStack() as ctx:
        def sb(name, shape, dt=fp32):
            return ctx.enter_context(nc.sbuf_tensor(name, shape, dt))

        def sem(name):
            return ctx.enter_context(nc.semaphore(name))

        wconv, w1, w2 = sb("wconv", [128, C]), sb("w1", [128, HIDDEN]), sb("w2", [128, HB, C])
        averager = sb("averager", [128, 32])
        square1, square2 = sb("square1", [128, PIXELS]), sb("square2", [128, PIXELS])
        sums = sb("sums", [128, HALF])
        rms_in, rms_out = sb("rms_in", [128, 16]), sb("rms_out", [128, 16])
        eps = sb("eps", [128, 16])
        mean_eps, neg_half = sb("mean_eps", [128, 16]), sb("neg_half2", [128, 16])
        inv_rms1, inv_rms2 = sb("inv_rms1", [128, PIXELS]), sb("inv_rms2", [128, PIXELS])
        normed1, act1 = sb("normed1", [128, PIXELS]), sb("act1", [128, PIXELS])
        normed2, act2 = sb("normed2", [128, PIXELS]), sb("act2", [128, NT, HB, HALF])
        result = sb("result", [128, PIXELS])
        psum = ctx.enter_context(nc.psum_tensor("psum2", [128, 8, HALF], fp32))

        weights_in, setup_done = sem("weights2_in"), sem("setup2_done")
        squares1, squares2, sums_ready, sums_taken = (
            sem("squares1"), sem("squares2"), sem("sums_ready"), sem("sums_taken"))
        rms_in_done, mean_ready, rms_ready, rms_stored, inv1_in, inv2_in = (
            sem("rms_in_done"), sem("mean_ready"), sem("rms_ready"), sem("rms_stored"), sem("inv1_in"), sem("inv2_in"))
        norm_step, normed1_ready, normed2_ready, act1_ready = (
            sem("norm_step"), sem("normed1_ready"), sem("normed2_ready"), sem("act1_ready"))
        conv_ready, conv_taken, hidden_ready, act2_ready, ffn_ready, result_ready, result_out = (
            sem("conv_ready"), sem("conv_taken"), sem("hidden_ready"), sem("act2_ready"), sem("ffn_ready"),
            sem("result_ready"), sem("result_out"))

        def run(eng, slot):
            for c in range(-FIRST, 1):
                slot(c)
            with eng.Fori(1, IMAGES - FIRST) as c:
                slot(c)
            for c in range(IMAGES - FIRST, IMAGES):
                slot(c)

        def image(b, lo=0, n=PIXELS):
            return x[:, one(b), lo:lo + n].squeeze(1)

        block = ctx.enter_context(nc.Block())

        @block.sync
        def _(sp):
            sp.dma_start(wconv[:, :], d["wconv"]).then_inc(weights_in, 16)
            sp.dma_start(w1[:, :], d["w1"]).then_inc(weights_in, 16)
            sp.dma_start(w2[:, :, :], d["w2"]).then_inc(weights_in, 16)

            def slot(c):
                made, stored = held(sp, c + (FIRST + 1)), held(sp, c * 16 + 16 * (FIRST + 1))
                used2, used1 = held(sp, c + CONV), held(sp, c + FIRST)
                if norms(c):
                    sp.wait_ge(sums_taken, made)
                    for g in range(4):
                        sp.dma_start(rms_in[32 * g:32 * g + 32, :], sums[32 * g:32 * g + 1, :].rearrange(
                            "o (k f) -> o k f", k=32)).then_inc(rms_in_done, 16)
                    sp.wait_ge(rms_ready, made)
                    sp.dma_start(d["rms"].rearrange("a (k f) -> (a k) f", f=16), rms_out[:, :]).then_inc(rms_stored, 16)
                    sp.wait_ge(rms_stored, stored)
                    if has_image(c + CONV):
                        at_least(sp, normed2_ready, used2)
                        sp.dma_start(inv_rms2[:, :], d["rms"][0:1, :].broadcast_to([128, PIXELS])).then_inc(inv2_in, 16)
                    if has_image(c + FIRST):
                        at_least(sp, normed1_ready, used1)
                        sp.dma_start(inv_rms1[:, :], d["rms"][1:2, :].broadcast_to([128, PIXELS])).then_inc(inv1_in, 16)

            run(sp, slot)

        @block.gpsimd
        def _(pool):
            nc.gpsimd.memset(neg_half[:, :], -0.5).then_inc(setup_done, 1)
            nc.gpsimd.memset(eps[:, :], RMS_EPS).then_inc(setup_done, 1)
            pool.wait_ge(setup_done, 3)

            def slot(c):
                if norms(c):
                    pool.wait_ge(rms_in_done, c * 64 + 64 * (FIRST + 1))
                    at_least(pool, rms_stored, c * 16 + 16 * FIRST)
                    nc.gpsimd.tensor_tensor(out=mean_eps[:, :], in0=rms_in[:, :], in1=eps[:, :],
                                            op=ALU.add).then_inc(mean_ready, 1)
                    pool.wait_ge(mean_ready, c + (FIRST + 1))
                    nc.gpsimd.tensor_tensor(out=rms_out[:, :], in0=mean_eps[:, :], in1=neg_half[:, :],
                                            op=ALU.pow).then_inc(rms_ready, 1)
            run(pool, slot)

        @block.tensor
        def _(pe):
            def convolve(c, t):
                if t == 0:
                    pe.wait_ge(act1_ready, c + 1)
                    at_least(pe, conv_taken, c * NT)
                else:
                    pe.wait_ge(conv_taken, c * NT + 1)
                nc.tensor.matmul(psum[:, 6, :], wconv[:, :], act1[:, HALF * t:HALF * t + HALF],
                                 start=True, stop=True).then_inc(conv_ready, 1)

            def hidden(c, t):
                for m in range(HB):
                    if t == 0 and m == 0:
                        pe.wait_ge(normed2_ready, c + 1)
                    at_least(pe, act2_ready, c * (NT * HB) + (t * HB + m - 3))
                    nc.tensor.matmul(psum[:, m, :], w1[:, 128 * m:128 * m + 128], normed2[:, HALF * t:HALF * t + HALF],
                                     start=True, stop=True).then_inc(hidden_ready, 1)

            def down(c, t):
                at_least(pe, result_ready, c * NT + (t - 1))
                for m in range(HB):
                    pe.wait_ge(act2_ready, c * (NT * HB) + (t * HB + m + 1))
                    mm = nc.tensor.matmul(psum[:, 4 + t, :], w2[:, m, :], act2[:, t, m, :],
                                          start=(m == 0), stop=(m == HB - 1))
                mm.then_inc(ffn_ready, 1)

            def sum_squares(c):
                at_least(pe, sums_taken, c + FIRST)
                sources = [(square2, squares2, c + CONV), (square1, squares1, c + FIRST)]
                if not has_image(c + CONV):
                    sources[0] = sources[1]
                if not has_image(c + FIRST):
                    sources[1] = sources[0]
                for g in range(4):
                    square, ready, b = sources[g // 2]
                    if g % 2 == 0:
                        pe.wait_ge(ready, b + 1)
                    t = g % 2
                    mm = nc.tensor.matmul(psum[32 * g:32 * g + 32, 7, :], averager[:, :],
                                          square[:, HALF * t:HALF * t + HALF], start=True, stop=True)
                mm.then_inc(sums_ready, 1)

            pe.wait_ge(weights_in, 48)
            pe.wait_ge(setup_done, 3)

            def slot(c):
                if has_image(c + CONV):
                    convolve(c + CONV, 0)
                if has_image(c):
                    hidden(c, 0)
                if has_image(c + CONV):
                    convolve(c + CONV, 1)
                if has_image(c):
                    down(c, 0)
                    hidden(c, 1)
                if norms(c):
                    sum_squares(c)
                if has_image(c):
                    down(c, 1)
            run(pe, slot)

        @block.scalar
        def _(act):
            def gelu_hidden(c, t):
                for m in range(HB):
                    act.wait_ge(hidden_ready, c * (NT * HB) + (t * HB + m + 1))
                    if m == 0:
                        at_least(act, ffn_ready, c * NT + (t - 1))
                    nc.scalar.activation(act2[:, t, m, :], psum[:, m, :], ACT.Gelu,
                                         bias=params[:, FFN_B1 + m:FFN_B1 + m + 1]).then_inc(act2_ready, 1)

            def store(c):
                act.wait_ge(result_ready, c * NT + NT)
                settled(act, weights_in, 48)
                act.dma_start(d["out"][one(c)].squeeze(0), result[:, :]).then_inc(result_out, 16)

            def slot(c):
                if has_image(c + CONV):
                    act.wait_ge(normed1_ready, c + (CONV + 1))
                    at_least(act, conv_ready, (c + CONV) * NT)
                    nc.scalar.activation(act1[:, :], normed1[:, :], ACT.Gelu).then_inc(act1_ready, 1)
                if has_image(c + FIRST):
                    at_least(act, sums_ready, c + FIRST)
                    nc.scalar.activation(square1[:, :], image(c + FIRST), ACT.Square).then_inc(squares1, 1)
                if has_image(c - 1):
                    store(c - 1)
                if has_image(c):
                    gelu_hidden(c, 0)
                if has_image(c + CONV):
                    act.wait_ge(conv_taken, (c + CONV) * NT + NT)
                    at_least(act, sums_ready, c + FIRST)
                    nc.scalar.activation(square2[:, :], image(c + CONV), ACT.Square).then_inc(squares2, 1)
                if has_image(c):
                    gelu_hidden(c, 1)
            run(act, slot)
            store(IMAGES - 1)
            act.wait_ge(result_out, 16 * IMAGES)

        @block.vector
        def _(dve):
            nc.vector.memset(averager[:, :], 1.0 / C).then_inc(setup_done, 1)
            dve.wait_ge(weights_in, 48)

            def slot(c):
                if has_image(c + CONV):
                    for t in range(NT):
                        dve.wait_ge(conv_ready, (c + CONV) * NT + (t + 1))
                        half = image(c + CONV, HALF * t, HALF)
                        nc.vector.scalar_tensor_tensor(out=half, in0=psum[:, 6, :], scalar=params[:, CONV_B:CONV_B + 1],
                                                       in1=half, op0=ALU.add, op1=ALU.add).then_inc(conv_taken, 1)
                if has_image(c):
                    output_half(c, 0)
                if norms(c):
                    dve.wait_ge(sums_ready, c + (FIRST + 1))
                    at_least(dve, rms_in_done, c * 64 + 64 * FIRST)
                    nc.vector.tensor_copy(sums[:, :], psum[:, 7, :]).then_inc(sums_taken, 1)
                if has_image(c + CONV - 1):
                    dve.wait_ge(inv2_in, (c + CONV) * 16)
                    at_least(dve, hidden_ready, (c + CONV - 1) * (NT * HB))
                    nc.vector.scalar_tensor_tensor(out=normed2[:, :], in0=image(c + CONV - 1),
                                                   scalar=params[:, RMS2_W:RMS2_W + 1],
                                                   in1=inv_rms2[:, :], op0=ALU.mult, op1=ALU.mult).then_inc(normed2_ready, 1)
                if has_image(c + FIRST - 1):
                    dve.wait_ge(inv1_in, (c + FIRST) * 16)
                    at_least(dve, act1_ready, c + (FIRST - 1))
                    nc.vector.scalar_tensor_tensor(out=normed1[:, :], in0=image(c + FIRST - 1),
                                                   scalar=params[:, RMS1_W:RMS1_W + 1],
                                                   in1=inv_rms1[:, :], op0=ALU.mult, op1=ALU.mult).then_inc(normed1_ready, 1)
                if has_image(c):
                    output_half(c, 1)

            def output_half(c, t):
                dve.wait_ge(ffn_ready, c * NT + t + 1)
                if t == 0:
                    at_least(dve, result_out, c * 16)
                nc.vector.scalar_tensor_tensor(out=result[:, HALF * t:HALF * t + HALF], in0=psum[:, 4 + t, :],
                                               scalar=params[:, FFN_B2:FFN_B2 + 1], in1=image(c, HALF * t, HALF),
                                               op0=ALU.add, op1=ALU.add).then_inc(result_ready, 1)
            run(dve, slot)


def norms(c):
    return has_image(c + CONV) or has_image(c + FIRST)


def build(nc, d):
    fp32 = mybir.dt.float32
    with nc.sbuf_tensor("x_sb", [128, IMAGES, PIXELS], fp32) as x, nc.sbuf_tensor("params_sb", [128, PARAMS], fp32) as params:
        attention_block(nc, x, params, d)
        ffn_block(nc, x, params, d)


def kernel(x, L0_conv_norm_w, L0_conv_norm_b, L0_conv_qkv_w, L0_conv_qkv_b, L0_conv_proj_w, L0_conv_proj_b,
           L1_conv_norm1_w, L1_conv_conv_w, L1_conv_conv_b, L1_conv_norm2_w, L1_conv_ffn_w1, L1_conv_ffn_b1,
           L1_conv_ffn_w2, L1_conv_ffn_b2):
    import numpy as np
    import concourse.bacc as bacc
    from concourse.bass_utils import run_bass_kernel_spmd

    def flat(a):
        return np.asarray(a).reshape(-1)

    qkv_w = np.asarray(L0_conv_qkv_w).reshape(2, 2, 2, 3, CH, C)
    qkv_b = np.asarray(L0_conv_qkv_b).reshape(2, 2, 2, 3, CH)
    split_w = qkv_w.transpose(3, 5, 0, 2, 4, 1).reshape(3, C, C)
    split_b = qkv_b.transpose(3, 0, 2, 4, 1).reshape(3, C)
    value_w = qkv_w[:, :, :, 2].transpose(4, 0, 1, 2, 3).reshape(C, C)
    value_b = qkv_b[:, :, :, 2].reshape(C)
    group = np.arange(C) // (C // GROUPS)
    columns = [None] * PARAMS
    for at, v in ((NORM_W, L0_conv_norm_w), (NORM_B, L0_conv_norm_b), (Q_B, split_b[0]), (K_B, split_b[1]), (V_B, value_b),
                  (PROJ_B, L0_conv_proj_b), (RMS1_W, L1_conv_norm1_w), (CONV_B, L1_conv_conv_b),
                  (RMS2_W, L1_conv_norm2_w), (FFN_B2, L1_conv_ffn_b2)):
        columns[at] = flat(v)
    for m in range(HB):
        columns[FFN_B1 + m] = flat(L1_conv_ffn_b1)[128 * m:128 * m + 128]
    arrays = {
        "x": np.asarray(x).reshape(IMAGES, C, PIXELS),
        "params": np.stack(columns, axis=1),
        "wq": split_w[0], "wk": split_w[1], "wv": value_w,
        "wp": np.asarray(L0_conv_proj_w).T,
        "group_mean": np.where(group[:, None] == group[None, :], np.float32(GROUPS / C), np.float32(0)).astype(np.float32),
        "identity": np.eye(C, dtype=np.float32),
        "wconv": np.asarray(L1_conv_conv_w).T,
        "w1": np.asarray(L1_conv_ffn_w1).T,
        "w2": np.asarray(L1_conv_ffn_w2).reshape(C, HB, 128).transpose(2, 1, 0),
    }
    arrays = {k: np.ascontiguousarray(v) for k, v in arrays.items()}
    nc = bacc.Bacc("TRN2", target_bir_lowering=False, num_devices=1)
    fp32 = mybir.dt.float32
    d = {k: nc.dram_tensor(f"in_{k}", v.shape, fp32, kind="ExternalInput").ap() for k, v in arrays.items()}
    d["out"] = nc.dram_tensor("out", (IMAGES, C, PIXELS), fp32, kind="ExternalOutput").ap()
    d["inv"] = nc.dram_tensor("inv_den_rows", (HEADS, PIXELS), fp32, kind="Internal").ap()
    d["rms"] = nc.dram_tensor("inv_rms_rows", (2, PIXELS), fp32, kind="Internal").ap()
    build(nc, d)
    r = run_bass_kernel_spmd(nc, [{f"in_{k}": v for k, v in arrays.items()}], core_ids=[0])
    return r.results[0]["out"].reshape(IMAGES, C, 32, 32)
```

```python
import concourse.bass as bass
from concourse import mybir
from contextlib import ExitStack

IMAGES, C, PIXELS = 16, 128, 1024
HEADS, GROUPS, HIDDEN = 8, 32, 512
CH = C // HEADS
HALF = 512
NT = PIXELS // HALF
NK = PIXELS // 128
UNIT_HEADS = 4
UNITS = IMAGES * HEADS // UNIT_HEADS
STEPS = NT * NK
RING = 4
ROWS = 64
MAX_ROW = ROWS - 2
LEAD = 6
BANKS = 3
TILES = 4 * STEPS
GN_EPS, RMS_EPS = 1e-5, 1e-8
STACK_DMAS, ROW_DMAS, HEAD_DMAS, WEIGHT_DMAS = 12, 8, 8, 7
SCALE = 1.0 / CH ** 0.5
HB = HIDDEN // 128
CONV, FIRST = 2, 4
(NORM_W, NORM_B, Q_B, K_B, PROJ_B, RMS1_W, CONV_B, RMS2_W, FFN_B2, V_B, FFN_B1) = range(11)
PARAMS = FFN_B1 + HB


def at_least(eng, sem, value):
    if isinstance(value, int) and value <= 0:
        return
    eng.wait_ge(sem, value)


def settled(eng, sem, value):
    eng.wait_ge(sem, value)


def held(eng, value):
    if not is_number(value):
        eng.compute_val(value)
    return value


def is_number(v):
    return isinstance(v, int)


def score_head(k):
    return 2 * (k // 2) + 1 - k % 2


def images_until(b):
    return min(b + 1, IMAGES) if is_number(b) else b + 1


def is_first(b):
    return is_number(b) and b == 0


def has_image(b):
    return not is_number(b) or 0 <= b < IMAGES


def has_unit(u):
    return not is_number(u) or 0 <= u < UNITS


def one(b):
    return slice(b, b + 1) if is_number(b) else bass.ds(b, 1)


def early(c):
    return is_number(c) and c < 2 - FIRST


def norms(c):
    return has_image(c + CONV) or has_image(c + FIRST)


def build(nc, d):
    fp32, fp32r = mybir.dt.float32, mybir.dt.float32r
    ALU, ACT, AX = mybir.AluOpType, mybir.ActivationFunctionType, mybir.AxisListType
    with ExitStack() as ctx:
        def sb(name, shape, dt=fp32):
            return ctx.enter_context(nc.sbuf_tensor(name, shape, dt))

        def sem(name):
            return ctx.enter_context(nc.semaphore(name))

        x, params = sb("x_sb", [128, IMAGES, PIXELS]), sb("params_sb", [128, PARAMS])
        q_stack = sb("q_stack", [128, RING, 2, PIXELS], fp32r)
        k_stack = sb("k_stack", [128, RING, 2, PIXELS], fp32r)
        probs = sb("probs", [128, 8, HALF])
        values = sb("values", [128, 2, NK, HEADS, 32])
        hid = sb("hid", [128, PIXELS])
        q_full, k_full = sb("q_full", [128, PIXELS]), sb("k_full", [128, PIXELS])
        q_high, q_low = sb("q_high", [128, PIXELS], fp32r), sb("q_low", [128, PIXELS], fp32r)
        k_high, k_low = sb("k_high", [128, PIXELS], fp32r), sb("k_low", [128, PIXELS], fp32r)
        raw = sb("raw", [128, PIXELS])
        attn = sb("attn", [128, PIXELS])
        inv_den = sb("inv_den", [128, PIXELS])
        den = sb("den", [128, PIXELS // CH])
        inv = sb("inv", [128, PIXELS // CH])
        wq, wk, wv = sb("wq", [128, C]), sb("wk", [128, C]), sb("wv", [128, C])
        wp = sb("wp", [128, C])
        out_bias = sb("out_bias", [128, 1])
        group_mean, identity = sb("group_mean", [128, C]), sb("identity", [128, C])
        maxes = sb("maxes", [128, 32, 2])
        neg_max = sb("neg_max", [128, 32])
        row_full = sb("row_full", [32, 128])
        row_high, row_low = sb("row_high", [32, 128], fp32r), sb("row_low", [32, 128], fp32r)
        stats = sb("stats", [128, 2, 6])
        mean_var = sb("mean_var", [128, 2])
        gn = sb("gn", [128, 12])
        g_mean, g_dev, g_square, g_mix, g_var, g_rstd, g_scale, g_tmp, g_shift, gn_eps, neg_half, settle = (
            gn[:, i:i + 1] for i in range(12))

        wconv = sb("wconv", [128, C])
        wconv_high, wconv_low = sb("wconv_high", [128, C], fp32r), sb("wconv_low", [128, C], fp32r)
        w1_high, w1_low = q_high[:, 0:HIDDEN], q_low[:, 0:HIDDEN]
        square1, square2, normed2 = k_full[:, :], hid[:, :], q_full[:, :]
        normed1, act1 = k_high[:, :].bitcast(fp32), k_low[:, :].bitcast(fp32)
        act1_high, act1_low, normed2_high, normed2_low = (q_stack[:, place, i, :] for place in range(2) for i in range(2))
        old_values = values[:, 0, :, :, :].rearrange("p k h i -> p (k h i)")
        inv_rms1, sums = old_values[:, 0:PIXELS], old_values[:, PIXELS:PIXELS + HALF]
        inv_rms2, w12, result = raw[:, :], inv_den[:, :], attn[:, :]

        def act2(t, m):
            return probs[:, HB * t + m, :]

        averager = sb("averager", [128, 32])
        rms_in, rms_out, mean_eps, eps, neg_halves = (sb(name, [128, 16]) for name in (
            "rms_in", "rms_out", "mean_eps", "eps", "neg_halves"))

        psum = ctx.enter_context(nc.psum_tensor("psum", [128, 8, HALF], fp32))
        acc, misc = psum[:, 6, :], psum[:, 7, :]
        HIDDEN_BANKS, CONV_BANKS, SUMS_BANK, OUT_BANK = (0, 1, 2, 7), (3, 4), 5, 6

        def steps_of(part):
            return {None: range(STEPS), 0: range(2), 1: range(2, 6), 2: range(6, 10), 3: range(10, STEPS)}[part]

        def fills(b):
            return is_number(b) and b == -2

        def qk_bank(b, n):
            return psum[:, n, :] if fills(b) else misc

        weights_in, x_in = sem("weights_in"), [sem(f"x_in{n}") for n in range(4)]
        x_rest_in = sem("x_rest_in")
        setup_done, stacks_set = sem("setup_done"), sem("stacks_set")
        stack_in, rows_in = sem("stack_in"), sem("rows_in")
        heads_in, inv_out, inv_in = sem("heads_in"), sem("inv_out"), sem("inv_in")
        stats_ready, gn_stats, gn_mean, gn_mix, gn_group, gn_var = (
            sem("stats_ready"), sem("gn_stats"), sem("gn_mean"), sem("gn_mix"), sem("gn_group"), sem("gn_var"))
        gn_scaled = sem("gn_scaled")
        hid_ready, qk_ready, qk_full, split_done = (
            sem("hid_ready"), sem("qk_ready"), sem("qk_full"), sem("split_done"))
        v_ready, v_full = sem("v_ready"), sem("v_full")
        max_ready, max_taken, neg_max_ready, max_turned, rows_ready = (
            sem("max_ready"), sem("max_taken"), sem("neg_max_ready"), sem("max_turned"), sem("rows_ready"))
        scores_ready, probs_ready, pv_done, acc_taken = (
            sem("scores_ready"), sem("probs_ready"), sem("pv_done"), sem("acc_taken"))
        inv_ready, attn_ready, proj_ready, proj_taken = (
            sem("inv_ready"), sem("attn_ready"), sem("proj_ready"), sem("proj_taken"))
        row_high_ready = sem("row_high_ready")
        bias_ready, bias_taken = sem("bias_ready"), sem("bias_taken")
        mean_taken = sem("mean_taken")
        gn_step, added = sem("gn_step"), sem("added")

        ffn_weights_in, ffn_setup = sem("ffn_weights_in"), sem("ffn_setup")
        squares1, squares2, sums_ready, sums_taken = (
            sem("squares1"), sem("squares2"), sem("sums_ready"), sem("sums_taken"))
        rms_in_done, mean_ready, rms_ready, rms_stored, inv1_in, inv2_in = (
            sem("rms_in_done"), sem("mean_ready"), sem("rms_ready"), sem("rms_stored"), sem("inv1_in"), sem("inv2_in"))
        weights_rounded, weights_split = sem("weights_rounded"), sem("weights_split")
        normed1_ready, normed2_ready = sem("normed1_ready"), sem("normed2_ready")
        act1_rounded, act1_split, normed2_rounded, normed2_split = (
            sem("act1_rounded"), sem("act1_split"), sem("normed2_rounded"), sem("normed2_split"))
        conv_ready, conv_taken, hidden_ready, act2_ready, ffn_ready, result_ready, result_out = (
            sem("conv_ready"), sem("conv_taken"), sem("hidden_ready"), sem("act2_ready"), sem("ffn_ready"),
            sem("result_ready"), sem("result_out"))

        def run(eng, slot, refine, activate=lambda c: None):
            def image(b, parity):
                for half in range(2):
                    slot(b, parity, half)
            for b in range(-2, 2):
                image(b, b % 2)
            with eng.Fori(1, IMAGES // 2 - 1) as i:
                for parity in range(2):
                    image(i * 2 + parity, parity)
            image(IMAGES - 2, 0)
            slot(IMAGES - 1, 1, 0)
            refine(-4)
            for part in range(3):
                slot(IMAGES - 1, 1, 1, part)
            refine(-3)
            slot(IMAGES - 1, 1, 1, 3)
            slot(IMAGES, 0, 0, 0)
            activate(-3)
            slot(IMAGES, 0, 0, 1)
            refine(-2)
            slot(IMAGES, 0, 0, 2)
            refine(-1)
            slot(IMAGES, 0, 0, 3)
            refine(0)
            with eng.Fori(1, IMAGES - FIRST) as c:
                refine(c)
            for c in range(IMAGES - FIRST, IMAGES):
                refine(c)

        def max_item(u, parity, half, s):
            if s + LEAD < STEPS:
                return u + 1, (2 * parity + half + 1) % RING, s + LEAD
            return u + 2, (2 * parity + half + 2) % RING, s + LEAD - STEPS

        def image_of_x(b, lo=0, n=PIXELS):
            return x[:, one(b), lo:lo + n].squeeze(1)

        block = ctx.enter_context(nc.Block())

        @block.sync
        def _(sp):
            def load_x(b, signal):
                sp.dma_start(x[:, b, :], d["x"][b]).then_inc(signal, 16)

            def stack(q_rounded, rounded, split, parity, half):
                for ready, count, pieces in (
                        (qk_full, q_rounded, ((q_stack, 0, q_high), (q_stack, 1, q_high))),
                        (qk_full, rounded, ((k_stack, 0, k_high), (k_stack, 2, k_high))),
                        (split_done, split, ((q_stack, 2, q_low), (k_stack, 1, k_low)))):
                    sp.wait_ge(ready, count)
                    for dst, n, part in pieces:
                        for j in range(2):
                            rows = slice(64 * half + 32 * j, 64 * half + 32 * j + 32)
                            at = ROWS * j + CH * n
                            sp.dma_start(dst[at:at + CH, 2 * parity + half, :, :].bitcast(fp32),
                                         part[rows, :].bitcast(fp32)).then_inc(stack_in, 16)

            def maximum_rows(parity, half):
                for p in range(2):
                    for j in range(2):
                        head = 2 * p + j
                        for n, src in enumerate((row_high, row_low)):
                            at = ROWS * j + MAX_ROW + n
                            row = q_stack[at:at + 1, 2 * parity + half, p, :].bitcast(fp32)
                            sp.dma_start(row.rearrange("o (k f) -> o k f", f=128),
                                         src[NK * head:NK * head + NK, :].bitcast(fp32)).then_inc(rows_in, 16)

            def heads(half):
                for g in range(UNIT_HEADS):
                    h = UNIT_HEADS * half + g
                    rows = slice(CH * h, CH * h + CH)
                    sp.dma_start(attn[rows, :], raw[32 * g:32 * g + CH, :]).then_inc(heads_in, 16)
                    sp.dma_start(den[rows, :], raw[32 * g + CH:32 * g + CH + 1, :].rearrange(
                        "o (k f) -> o k f", k=CH)).then_inc(heads_in, 16)

            def slot(b, parity, half, part=None):
                u = b * 2 + half
                scored = held(sp, u * TILES)
                taken, placed = held(sp, u * NT), held(sp, (u - 1) * (16 * HEAD_DMAS))
                turned, rowed = held(sp, u + 2), held(sp, (u + 1) * (16 * ROW_DMAS))
                if half == 0:
                    q_rounded, rounded, split = held(sp, b * 4 + 6), held(sp, b * 4 + 8), held(sp, b * 2 + 4)
                    stacked = held(sp, (b + 1) * (2 * 16 * STACK_DMAS) + 16 * STACK_DMAS)
                    inverted, written, projected = held(sp, b), held(sp, b * 16), held(sp, (b - 1) * NT)
                else:
                    q_rounded, rounded, split = held(sp, b * 4 + 10), held(sp, b * 4 + 12), held(sp, b * 2 + 6)
                    stacked = held(sp, (b + 2) * (2 * 16 * STACK_DMAS))
                    inverted, projected = held(sp, b), held(sp, b * NT)
                if part in (2, 3):
                    return
                if half == 0 and has_image(b + 1):
                    at_least(sp, scores_ready, scored)
                    at_least(sp, stack_in, stacked)
                    stack(q_rounded, rounded, split, 1 - parity, 1)
                if has_unit(u - 1) and part in (None, 0):
                    at_least(sp, acc_taken, taken)
                    if half == 1:
                        at_least(sp, added, projected)
                        at_least(sp, inv_ready, inverted)
                    at_least(sp, heads_in, placed)
                    heads(1 - half)
                if is_first(b) and half == 0:
                    for n in range(4, IMAGES):
                        load_x(n, x_rest_in)
                if half == 0 and has_image(b - 1) and part in (None, 1):
                    sp.wait_ge(inv_ready, inverted)
                    at_least(sp, proj_ready, projected)
                    sp.dma_start(d["inv"].rearrange("h (k f) -> (h k) f", k=CH), inv[:, :]).then_inc(inv_out, 16)
                    sp.wait_ge(inv_out, written)
                    for h in range(HEADS):
                        sp.dma_start(inv_den[CH * h:CH * h + CH, :],
                                     d["inv"][h:h + 1, :].broadcast_to([CH, PIXELS])).then_inc(inv_in, 16)
                if half == 1 and has_image(b + 2):
                    at_least(sp, scores_ready, scored)
                    at_least(sp, stack_in, stacked)
                    stack(q_rounded, rounded, split, parity, 0)
                if has_unit(u + 1):
                    sp.wait_ge(rows_ready, turned)
                    at_least(sp, rows_in, rowed)
                    maximum_rows(parity if half == 0 else 1 - parity, 1 - half)

            def load_ffn_weights(c):
                if c == -FIRST:
                    sp.dma_start(wconv[:, :], d["wconv"]).then_inc(ffn_weights_in, 16)
                else:
                    sp.wait_ge(attn_ready, IMAGES)
                    sp.dma_start(w12, d["w12"]).then_inc(ffn_weights_in, 16)

            def refine(c):
                if is_number(c) and c in (-FIRST, -1):
                    load_ffn_weights(c)
                made, stored = held(sp, c + (FIRST + 1)), held(sp, c * 16 + 16 * (FIRST + 1))
                used2, used1 = held(sp, c + CONV), held(sp, c + FIRST)
                if norms(c):
                    sp.wait_ge(sums_taken, made)
                    for g in range(4):
                        sp.dma_start(rms_in[32 * g:32 * g + 32, :], sums[32 * g:32 * g + 1, :].rearrange(
                            "o (k f) -> o k f", k=32)).then_inc(rms_in_done, 16)
                    sp.wait_ge(rms_ready, made)
                    sp.dma_start(d["rms"].rearrange("a (k f) -> (a k) f", f=16), rms_out[:, :]).then_inc(rms_stored, 16)
                    sp.wait_ge(rms_stored, stored)
                    if has_image(c + FIRST):
                        at_least(sp, normed1_ready, used1)
                        sp.dma_start(inv_rms1, d["rms"][1:2, :].broadcast_to([128, PIXELS])).then_inc(inv1_in, 16)
                    if has_image(c + CONV):
                        at_least(sp, normed2_ready, used2)
                        sp.dma_start(inv_rms2, d["rms"][0:1, :].broadcast_to([128, PIXELS])).then_inc(inv2_in, 16)

            load_x(0, x_in[0])
            for tile, name in ((wq, "wq"), (wk, "wk"), (wv, "wv"), (wp, "wp"), (group_mean, "group_mean"),
                               (identity, "identity"), (params, "params")):
                sp.dma_start(tile[:, :], d[name]).then_inc(weights_in, 16)
            for n in range(1, 4):
                load_x(n, x_in[n])
            sp.wait_ge(stacks_set, 2)
            run(sp, slot, refine)

        @block.gpsimd
        def _(pool):
            def maximum_parts(turned):
                pool.wait_ge(row_high_ready, turned)
                at_least(pool, rows_in, (turned - 1) * (16 * ROW_DMAS))
                nc.gpsimd.tensor_tensor(out=row_low[:, :], in0=row_full[:, :], in1=row_high[:, :].bitcast(fp32),
                                        op=ALU.subtract).then_inc(rows_ready, 1)

            def group_statistics(b):
                step = (b + 2) * 5
                pool.wait_ge(mean_taken, b + 3)
                nc.gpsimd.tensor_tensor(out=g_dev, in0=mean_var[:, 0:1], in1=g_mean,
                                        op=ALU.subtract).then_inc(gn_step, 1)
                pool.wait_ge(gn_step, step + 1)
                nc.gpsimd.tensor_tensor(out=g_square, in0=g_dev, in1=g_dev, op=ALU.mult).then_inc(gn_step, 1)
                pool.wait_ge(gn_step, step + 2)
                nc.gpsimd.tensor_tensor(out=g_mix, in0=g_square, in1=mean_var[:, 1:2], op=ALU.add).then_inc(gn_mix, 1)

            def scale_and_shift(b):
                step = (b + 2) * 5
                pool.wait_ge(gn_var, b + 3)
                nc.gpsimd.tensor_tensor(out=g_rstd, in0=g_var, in1=neg_half, op=ALU.pow).then_inc(gn_step, 1)
                pool.wait_ge(gn_step, step + 3)
                at_least(pool, hid_ready, b + 2)
                nc.gpsimd.tensor_tensor(out=g_scale, in0=g_rstd, in1=params[:, NORM_W:NORM_W + 1],
                                        op=ALU.mult).then_inc(gn_step, 1)
                pool.wait_ge(gn_step, step + 4)
                nc.gpsimd.tensor_tensor(out=g_tmp, in0=g_mean, in1=g_scale, op=ALU.mult).then_inc(gn_step, 1)
                pool.wait_ge(gn_step, step + 5)
                nc.gpsimd.tensor_tensor(out=g_shift, in0=params[:, NORM_B:NORM_B + 1], in1=g_tmp,
                                        op=ALU.subtract).then_inc(gn_scaled, 1)

            def slot(b, parity, half, part=None):
                u = b * 2 + half
                if half == 0:
                    if has_image(b + 2):
                        group_statistics(b)
                        scale_and_shift(b)
                    if has_unit(u + 1):
                        maximum_parts(u + 2)
                    if has_image(b - 1) and part in (None, 2):
                        pool.wait_ge(inv_in, b * (16 * HEADS))
                        pool.wait_ge(heads_in, b * (2 * 16 * HEAD_DMAS))
                        nc.gpsimd.tensor_tensor(out=attn[:, :], in0=attn[:, :], in1=inv_den[:, :],
                                                op=ALU.mult).then_inc(attn_ready, 1)
                    if has_image(b - 1) and part in (None, 3):
                        for t in range(NT):
                            pool.wait_ge(proj_taken, (b - 1) * NT + (t + 1))
                            half_image = image_of_x(b - 1, HALF * t, HALF)
                            nc.gpsimd.tensor_tensor(out=half_image, in0=attn[:, HALF * t:HALF * t + HALF],
                                                    in1=half_image, op=ALU.add).then_inc(added, 1)
                if half == 1 and has_image(b + 2):
                    for full, high, low, made in ((q_full, q_high, q_low, 2), (k_full, k_high, k_low, 4)):
                        pool.wait_ge(qk_full, (b + 2) * 4 + made)
                        nc.gpsimd.tensor_tensor(out=low[:, :], in0=full[:, :], in1=high[:, :].bitcast(fp32),
                                                op=ALU.subtract).then_inc(split_done, 1)
                if half == 1 and has_unit(u + 1):
                    maximum_parts(u + 2)

            def refine(c):
                if norms(c):
                    pool.wait_ge(rms_in_done, c * 64 + 64 * (FIRST + 1))
                    at_least(pool, rms_stored, c * 16 + 16 * FIRST)
                    nc.gpsimd.tensor_tensor(out=mean_eps[:, :], in0=rms_in[:, :], in1=eps[:, :],
                                            op=ALU.add).then_inc(mean_ready, 1)
                    pool.wait_ge(mean_ready, c + (FIRST + 1))
                    nc.gpsimd.tensor_tensor(out=rms_out[:, :], in0=mean_eps[:, :], in1=neg_halves[:, :],
                                            op=ALU.pow).then_inc(rms_ready, 1)

            nc.gpsimd.memset(q_stack[:, :, :, :].bitcast(fp32), 0.0).then_inc(stacks_set, 1)
            pool.wait_ge(weights_in, 16 * WEIGHT_DMAS)
            pool.wait_ge(setup_done, 3)
            nc.gpsimd.memset(neg_halves[:, :], -0.5).then_inc(ffn_setup, 1)
            nc.gpsimd.memset(eps[:, :], RMS_EPS).then_inc(ffn_setup, 1)
            run(pool, slot, refine)

        @block.tensor
        def _(pe):
            def values_of(c, part):
                if part == 0:
                    pe.wait_ge(hid_ready, c + 1)
                for k in range(4):
                    chunk = 4 * part + k
                    last = nc.tensor.matmul(misc[:, 128 * k:128 * k + 128], hid[:, 128 * chunk:128 * chunk + 128],
                                            wv[:, :], start=True, stop=True)
                last.then_inc(v_ready, 1)

            def side_jobs(b, parity, half, s):
                u = b * 2 + half
                c = b + 2
                if s == 11 and has_unit(u + 1):
                    pe.wait_ge(neg_max_ready, u + 2)
                    at_least(pe, row_high_ready, u + 1)
                    if half == 0:
                        at_least(pe, v_full, images_until(b + 1) * 2)
                        at_least(pe, gn_var, images_until(b + 2))
                    else:
                        at_least(pe, qk_full, images_until(b + 2) * 4)
                    at_least(pe, proj_taken, images_until(b - 2 + half) * NT)
                    nc.tensor.transpose(misc[0:32, 0:128], neg_max[:, :], identity[:, :]).then_inc(max_turned, 1)
                if half == 0:
                    if s == 3 and (has_image(c) or has_image(b + 1)):
                        at_least(pe, row_high_ready, u + 1)
                        at_least(pe, qk_full, images_until(b + 1) * 4)
                    if s == 3 and has_image(c):
                        pe.wait_ge(gn_stats, b + 3)
                        nc.tensor.matmul(misc[:, 0:1], group_mean[:, :], mean_var[:, 0:1],
                                         start=True, stop=True).then_inc(gn_mean, 1)
                    if s == 4 and has_image(b + 1):
                        if has_image(c):
                            pe.wait_ge(mean_taken, b + 3)
                        values_of(b + 1, 0)
                    if s == 6 and has_image(b + 1):
                        pe.wait_ge(v_full, b * 2 + 3)
                        values_of(b + 1, 1)
                    if s == 9 and has_image(c):
                        at_least(pe, v_full, b * 2 + 4)
                        pe.wait_ge(gn_mix, b + 3)
                        nc.tensor.matmul(misc[:, 0:1], group_mean[:, :], g_mix, start=True, stop=True).then_inc(gn_group, 1)
                    if s in (13, 15) and has_image(b - 1):
                        t = (s - 13) // 2
                        if t == 0:
                            at_least(pe, row_high_ready, min(u + 2, UNITS) if is_number(u) else u + 2)
                            at_least(pe, proj_taken, (b - 1) * 2)
                            pe.wait_ge(attn_ready, b)
                        else:
                            pe.wait_ge(proj_taken, b * 2 - 1)
                        nc.tensor.matmul(misc, wp[:, :], attn[:, HALF * t:HALF * t + HALF],
                                         start=True, stop=True).then_inc(proj_ready, 1)
                elif s in (2, 4, 6, 8) and has_image(c):
                    n = (s - 2) // 2
                    if n == 0:
                        pe.wait_ge(hid_ready, b + 3)
                        at_least(pe, row_high_ready, u + 1)
                        at_least(pe, proj_taken, images_until(b - 1) * NT)
                    elif not fills(b):
                        pe.wait_ge(qk_full, b * 4 + (8 + n))
                    weight, t = ((wq, 0), (wq, 1), (wk, 0), (wk, 1))[n]
                    nc.tensor.matmul(qk_bank(b, n), weight[:, :], hid[:, HALF * t:HALF * t + HALF],
                                     start=True, stop=True).then_inc(qk_ready, 1)

            def wait_for_bank(before, tile, freed):
                if tile == 0:
                    at_least(pe, freed, before)
                elif tile >= BANKS:
                    at_least(pe, freed, before + (tile - BANKS + 1))

            def maximum_scores(u, parity, half, s, k):
                unit, place, step = max_item(u, parity, half, s)
                if not has_unit(unit):
                    return
                j, key_half, p, chunk, tile = k % 2, k // 2, step % 2, step // 2, 4 * s + k
                rows = slice(ROWS * j, ROWS * j + MAX_ROW)
                if step == 0 and k == 0:
                    pe.wait_ge(stack_in, unit * (16 * STACK_DMAS) + 16 * STACK_DMAS)
                wait_for_bank(u * TILES + (TILES + 4 * LEAD), tile, max_taken)
                nc.tensor.matmul(psum[:, BANKS + tile % BANKS, :], q_stack[rows, place, p, 128 * chunk:128 * chunk + 128],
                                 k_stack[rows, place, p, HALF * key_half:HALF * key_half + HALF],
                                 start=True, stop=True).then_inc(max_ready, 1)

            def scores(u, place, s, k):
                head, t, chunk, tile = score_head(k), s // NK, s % NK, 4 * s + k
                rows = slice(ROWS * (head % 2), ROWS * (head % 2) + ROWS)
                p = head // 2
                if tile == 0:
                    pe.wait_ge(rows_in, u * (16 * ROW_DMAS) + 16 * ROW_DMAS)
                wait_for_bank(u * TILES, tile, probs_ready)
                nc.tensor.matmul(psum[:, tile % BANKS, :], k_stack[rows, place, p, 128 * chunk:128 * chunk + 128],
                                 q_stack[rows, place, p, HALF * t:HALF * t + HALF],
                                 start=True, stop=True).then_inc(scores_ready, 1)

            def weigh_values(u, parity, half, s):
                chunk = s % NK
                pe.wait_ge(probs_ready, u * TILES + (4 * s + 4))
                if chunk == 0:
                    at_least(pe, acc_taken, u * NT + s // NK)
                if s == 0 and half == 0:
                    pe.wait_ge(v_full, u + 2)
                for k in range(UNIT_HEADS):
                    g = score_head(k)
                    last = nc.tensor.matmul(acc[32 * g:32 * g + 32, :],
                                            values[:, parity, chunk, UNIT_HEADS * half + g, :],
                                            probs[:, (4 * s + k) % 8, :],
                                            start=(chunk == 0), stop=(chunk == NK - 1))
                last.then_inc(pv_done, 1)

            def slot(b, parity, half, part=None):
                u = b * 2 + half
                for s in steps_of(part):
                    side_jobs(b, parity, half, s)
                    for k in range(4):
                        maximum_scores(u, parity, half, s, k)
                        if has_unit(u):
                            scores(u, 2 * parity + half, s, k)
                    if s == 0:
                        if has_unit(u - 1):
                            if half == 0:
                                weigh_values(u - 1, 1 - parity, 1, STEPS - 1)
                            else:
                                weigh_values(u - 1, parity, 0, STEPS - 1)
                    elif has_unit(u):
                        weigh_values(u, parity, half, s - 1)

            def product(out, weights, high, low):
                w_high, w_low = weights
                nc.tensor.matmul(out, w_high, high, start=True, stop=False)
                nc.tensor.matmul(out, w_high, low, start=False, stop=False)
                return nc.tensor.matmul(out, w_low, high, start=False, stop=True)

            def convolve(c, t):
                if t == 0:
                    pe.wait_ge(act1_split, c + 1)
                at_least(pe, conv_taken, c * NT + (t - 1))
                half = slice(HALF * t, HALF * t + HALF)
                product(psum[:, CONV_BANKS[t], :], (wconv_high[:, :], wconv_low[:, :]),
                        act1_high[:, half], act1_low[:, half]).then_inc(conv_ready, 1)

            def hidden(c, t):
                half = slice(HALF * t, HALF * t + HALF)
                for m in range(HB):
                    if t == 0 and m == 0:
                        pe.wait_ge(normed2_split, c + 1)
                    at_least(pe, act2_ready, c * (NT * HB) + (t * HB + m - 3))
                    features = slice(128 * m, 128 * m + 128)
                    product(psum[:, HIDDEN_BANKS[m], :], (w1_high[:, features], w1_low[:, features]),
                            normed2_high[:, half], normed2_low[:, half]).then_inc(hidden_ready, 1)

            def down(c, t):
                at_least(pe, result_ready, c * NT + t)
                for m in range(HB):
                    pe.wait_ge(act2_ready, c * (NT * HB) + (t * HB + m + 1))
                    at = HIDDEN + 128 * m
                    mm = nc.tensor.matmul(psum[:, OUT_BANK, :], w12[:, at:at + 128], act2(t, m),
                                          start=(m == 0), stop=(m == HB - 1))
                mm.then_inc(ffn_ready, 1)

            def sum_squares(c):
                at_least(pe, sums_taken, c + FIRST)
                sources = [(square2, squares2, c + CONV), (square1, squares1, c + FIRST)]
                if not has_image(c + CONV):
                    sources[0] = sources[1]
                if not has_image(c + FIRST):
                    sources[1] = sources[0]
                for g in range(4):
                    square, ready, b = sources[g // 2]
                    if g % 2 == 0:
                        pe.wait_ge(ready, b + 1)
                    t = g % 2
                    mm = nc.tensor.matmul(psum[32 * g:32 * g + 32, SUMS_BANK, :], averager[:, :],
                                          square[:, HALF * t:HALF * t + HALF], start=True, stop=True)
                mm.then_inc(sums_ready, 1)


            def refine(c):
                if is_number(c) and c == -FIRST:
                    pe.wait_ge(ffn_setup, 3)
                    pe.wait_ge(max_taken, UNITS * TILES)
                if is_number(c) and c == -CONV:
                    pe.wait_ge(weights_split, 1)
                if is_number(c) and c == 0:
                    pe.wait_ge(weights_split, 2)
                    pe.wait_ge(probs_ready, UNITS * TILES)
                    pe.wait_ge(acc_taken, UNITS * NT)
                    pe.wait_ge(proj_taken, IMAGES * NT)
                if has_image(c + CONV):
                    convolve(c + CONV, 0)
                    convolve(c + CONV, 1)
                if has_image(c):
                    hidden(c, 0)
                if norms(c):
                    sum_squares(c)
                if has_image(c):
                    down(c, 0)
                    hidden(c, 1)
                    down(c, 1)

            pe.wait_ge(weights_in, 16 * WEIGHT_DMAS)
            pe.wait_ge(setup_done, 3)
            nc.tensor.matmul(misc[:, 0:1], wp[:, :], params[:, V_B:V_B + 1], start=True, stop=True).then_inc(bias_ready, 1)
            pe.wait_ge(bias_taken, 1)
            run(pe, slot, refine)

        @block.scalar
        def _(act):
            def side_jobs(b, parity, half, s, k):
                u = b * 2 + half
                if s % NK == 1 and k == 0 and has_unit(u if s > 1 else u - 1):
                    t = 0 if s > 1 else 1
                    v = u if s > 1 else u - 1
                    act.wait_ge(pv_done, v * STEPS + NK * (t + 1))
                    at_least(act, heads_in, v * (16 * HEAD_DMAS))
                    nc.scalar.copy(raw[:, HALF * t:HALF * t + HALF], acc).then_inc(acc_taken, 1)
                if s == 11 and k == 0 and has_unit(u + 1):
                    act.wait_ge(max_turned, u + 2)
                    at_least(act, rows_ready, u + 1)
                    at_least(act, rows_in, (u + 1) * (16 * ROW_DMAS))
                    nc.scalar.copy(row_full[:, :], misc[0:32, 0:128])
                    nc.scalar.copy(row_high[:, :], misc[0:32, 0:128]).then_inc(row_high_ready, 1)
                if half == 0 and s == 3 and k == 0 and has_image(b + 2):
                    act.wait_ge(gn_mean, b + 3)
                    at_least(act, gn_scaled, b + 2)
                    nc.scalar.copy(g_mean, misc[:, 0:1]).then_inc(mean_taken, 1)
                if half == 0 and s == 9 and k == 0 and has_image(b + 2):
                    act.wait_ge(gn_group, b + 3)
                    nc.scalar.activation(g_var, misc[:, 0:1], ACT.Identity, bias=gn_eps).then_inc(gn_var, 1)
                if half == 0 and s in (4, 6) and k == 3 and has_image(b + 1):
                    part = (s - 4) // 2
                    act.wait_ge(v_ready, b * 2 + 3 + part)
                    at_least(act, pv_done, u * STEPS)
                    nc.scalar.copy(values[:, 1 - parity, 4 * part:4 * part + 4, :, 0:CH],
                                   misc.rearrange("p (k h i) -> p k h i", k=4, i=CH)).then_inc(v_full, 1)
                if half == 0 and s in (13, 15) and k == 3 and has_image(b - 1):
                    t = (s - 13) // 2
                    act.wait_ge(proj_ready, (b - 1) * NT + (t + 1))
                    nc.scalar.activation(attn[:, HALF * t:HALF * t + HALF], misc, ACT.Identity,
                                         bias=out_bias[:, :]).then_inc(proj_taken, 1)
                if half == 0 and s in (12, 14) and k == 3 and has_image(b + 2):
                    t = (s - 12) // 2
                    act.wait_ge(gn_scaled, b + 3)
                    at_least(act, v_ready, (b + 2) * 2)
                    last = nc.scalar.activation(hid[:, HALF * t:HALF * t + HALF], image_of_x(b + 2, HALF * t, HALF),
                                                ACT.Identity, bias=g_shift, scale=g_scale)
                    if t == 1:
                        last.then_inc(hid_ready, 1)
                if half == 1 and s in (2, 4, 6, 8) and k == 3 and has_image(b + 2):
                    n = (s - 2) // 2
                    act.wait_ge(qk_ready, b * 4 + (9 + n))
                    if n == 0:
                        at_least(act, split_done, (b + 2) * 2)
                        at_least(act, stack_in, (b + 2) * (2 * 16 * STACK_DMAS))
                    full, high, bias = ((q_full, q_high, Q_B), (k_full, k_high, K_B))[n // 2]
                    half_image = slice(HALF * (n % 2), HALF * (n % 2) + HALF)
                    for out in (full, high):
                        last = nc.scalar.activation(out[:, half_image], qk_bank(b, n), ACT.Identity,
                                                    bias=params[:, bias:bias + 1])
                    last.then_inc(qk_full, 1)

            def slot(b, parity, half, part=None):
                u = b * 2 + half
                for s in steps_of(part):
                    for k in range(UNIT_HEADS):
                        if has_unit(u):
                            tile = 4 * s + k
                            act.wait_ge(scores_ready, u * TILES + (tile + 1))
                            if k == 0:
                                at_least(act, pv_done, u * STEPS + (s - 1))
                            nc.scalar.activation(probs[:, tile % 8, :], psum[:, tile % BANKS, :],
                                                 ACT.Exp, scale=SCALE).then_inc(probs_ready, 1)
                        side_jobs(b, parity, half, s, k)

            def gelu_hidden(c, t):
                for m in range(HB):
                    act.wait_ge(hidden_ready, c * (NT * HB) + (t * HB + m + 1))
                    if m == 0:
                        at_least(act, ffn_ready, c * NT + (t - 1))
                    nc.scalar.activation(act2(t, m), psum[:, HIDDEN_BANKS[m], :], ACT.Gelu,
                                         bias=params[:, FFN_B1 + m:FFN_B1 + m + 1]).then_inc(act2_ready, 1)

            def store(c):
                act.wait_ge(result_ready, c * NT + NT)
                settled(act, ffn_weights_in, 16)
                act.dma_start(d["out"][one(c)].squeeze(0), result).then_inc(result_out, 16)

            def activate(c):
                act.wait_ge(normed1_ready, c + FIRST)
                at_least(act, conv_ready, (c + FIRST - 1) * NT)
                at_least(act, act1_split, c + (FIRST - 1))
                nc.scalar.activation(act1, normed1, ACT.Gelu)
                nc.scalar.activation(act1_high, normed1, ACT.Gelu).then_inc(act1_rounded, 1)

            def refine(c):
                if is_number(c) and -FIRST + 1 < c <= 0:
                    act.wait_ge(added, (c + FIRST + 1 if c < 0 else IMAGES) * NT)
                if has_image(c + FIRST) and not early(c):
                    at_least(act, sums_ready, c + FIRST)
                    nc.scalar.activation(square1, image_of_x(c + FIRST), ACT.Square).then_inc(squares1, 1)
                if has_image(c - 1):
                    store(c - 1)
                if has_image(c + CONV):
                    act.wait_ge(conv_taken, (c + CONV) * NT + NT)
                    at_least(act, sums_ready, c + FIRST)
                    nc.scalar.activation(square2, image_of_x(c + CONV), ACT.Square).then_inc(squares2, 1)
                if has_image(c):
                    gelu_hidden(c, 0)
                if has_image(c + FIRST - 1) and not is_first(c + FIRST - 1):
                    activate(c)
                if has_image(c):
                    gelu_hidden(c, 1)
                if has_image(c + CONV - 1):
                    act.wait_ge(normed2_ready, c + CONV)
                    at_least(act, hidden_ready, (c + CONV - 1) * (NT * HB))
                    nc.scalar.copy(normed2_high, normed2).then_inc(normed2_rounded, 1)

            act.wait_ge(weights_in, 16 * WEIGHT_DMAS)
            act.wait_ge(setup_done, 3)
            run(act, slot, refine, activate)
            store(IMAGES - 1)
            act.wait_ge(result_out, 16 * IMAGES)

        @block.vector
        def _(dve):
            def take_maxima(u, parity, half, s):
                unit, _, step = max_item(u, parity, half, s)
                if not has_unit(unit):
                    return
                for k in range(4):
                    j, key_half, p, chunk = k % 2, k // 2, step % 2, step // 2
                    dve.wait_ge(max_ready, u * TILES + (TILES + 4 * (LEAD + s) + k + 1))
                    if step == 0 and k == 0:
                        at_least(dve, neg_max_ready, unit)
                    nc.vector.tensor_reduce(maxes[:, (2 * p + j) * NK + chunk, key_half:key_half + 1],
                                            psum[:, BANKS + (4 * s + k) % BANKS, :], axis=AX.X, op=ALU.max).then_inc(max_taken, 1)
                if step == STEPS - 1:
                    dve.wait_ge(max_taken, unit * TILES + TILES)
                    at_least(dve, max_turned, unit)
                    nc.vector.tensor_reduce(neg_max[:, :], maxes[:, :, :], axis=AX.X, op=ALU.max,
                                            negate=True).then_inc(neg_max_ready, 1)

            def side_jobs(b, parity, half, s):
                c = b + 2
                if half == 1:
                    return
                if s < NT and has_image(c):
                    t = s
                    if is_number(c):
                        dve.wait_ge(x_in[c], 16)
                    else:
                        dve.wait_ge(x_rest_in, 16 * (IMAGES - 4))
                    nc.vector.bn_stats(stats[:, t, :], image_of_x(c, HALF * t, HALF)).then_inc(stats_ready, 1)
                if s == 1 and has_image(c):
                    dve.wait_ge(stats_ready, b * 2 + 6)
                    at_least(dve, gn_mix, b + 2)
                    nc.vector.memset(settle, 0.0)
                    nc.vector.bn_aggr(mean_var[:, :], stats[:, :, :].rearrange("p a b -> p (a b)")).then_inc(gn_stats, 1)
                    if fills(b):
                        nc.vector.memset(k_stack[:, :, :, :].bitcast(fp32), 1.0).then_inc(stacks_set, 1)
                if s == 5 and has_image(b - 1):
                    dve.wait_ge(heads_in, b * (2 * 16 * HEAD_DMAS))
                    at_least(dve, inv_out, (b - 1) * 16)
                    nc.vector.reciprocal(inv[:, :], den[:, :]).then_inc(inv_ready, 1)

            def slot(b, parity, half, part=None):
                u = b * 2 + half
                if half == 0 and has_image(b + 2):
                    at_least(dve, gn_stats, b + 2)
                for s in steps_of(part):
                    take_maxima(u, parity, half, s)
                    side_jobs(b, parity, half, s)


            def split_weights(n, full, high, low):
                dve.wait_ge(ffn_weights_in, 16 * n)
                nc.vector.tensor_copy(high, full).then_inc(weights_rounded, 1)
                dve.wait_ge(weights_rounded, n)
                nc.vector.tensor_tensor(out=low, in0=full, in1=high.bitcast(fp32),
                                        op=ALU.subtract).then_inc(weights_split, 1)

            def convolved(c, t):
                dve.wait_ge(conv_ready, c * NT + (t + 1))
                half = image_of_x(c, HALF * t, HALF)
                nc.vector.scalar_tensor_tensor(out=half, in0=psum[:, CONV_BANKS[t], :], scalar=params[:, CONV_B:CONV_B + 1],
                                               in1=half, op0=ALU.add, op1=ALU.add).then_inc(conv_taken, 1)

            def activate(c):
                dve.wait_ge(act1_rounded, c + FIRST)
                nc.vector.tensor_tensor(out=act1_low, in0=act1, in1=act1_high.bitcast(fp32),
                                        op=ALU.subtract).then_inc(act1_split, 1)

            def refine(c):
                if early(c):
                    dve.wait_ge(added, (c + FIRST + 1) * NT)
                    dve.wait_ge(stack_in, UNITS * (16 * STACK_DMAS))
                    at_least(dve, sums_ready, c + FIRST)
                    whole = image_of_x(c + FIRST)
                    nc.vector.tensor_tensor(out=square1, in0=whole, in1=whole,
                                            op=ALU.mult).then_inc(squares1, 1)
                if has_image(c + CONV):
                    convolved(c + CONV, 0)
                    convolved(c + CONV, 1)
                if is_number(c) and c == -FIRST:
                    dve.wait_ge(pv_done, (UNITS - 2) * STEPS)
                if norms(c):
                    dve.wait_ge(sums_ready, c + (FIRST + 1))
                    at_least(dve, rms_in_done, c * 64 + 64 * FIRST)
                    nc.vector.tensor_copy(sums, psum[:, SUMS_BANK, :]).then_inc(sums_taken, 1)
                if is_number(c) and c == -FIRST:
                    split_weights(1, wconv[:, :], wconv_high[:, :], wconv_low[:, :])
                    dve.wait_ge(scores_ready, (UNITS - 2) * TILES)
                if has_image(c + FIRST - 1):
                    dve.wait_ge(inv1_in, (c + FIRST) * 16)
                    at_least(dve, act1_rounded, c + (FIRST - 1))
                    nc.vector.scalar_tensor_tensor(out=normed1, in0=image_of_x(c + FIRST - 1),
                                                   scalar=params[:, RMS1_W:RMS1_W + 1],
                                                   in1=inv_rms1, op0=ALU.mult, op1=ALU.mult).then_inc(normed1_ready, 1)
                if has_image(c + CONV - 1):
                    dve.wait_ge(inv2_in, (c + CONV) * 16)
                    at_least(dve, normed2_split, c + (CONV - 1))
                    nc.vector.scalar_tensor_tensor(out=normed2, in0=image_of_x(c + CONV - 1),
                                                   scalar=params[:, RMS2_W:RMS2_W + 1],
                                                   in1=inv_rms2, op0=ALU.mult, op1=ALU.mult).then_inc(normed2_ready, 1)
                if has_image(c):
                    output_half(c, 0)
                if has_image(c + FIRST - 1) and not is_first(c + FIRST - 1):
                    activate(c)
                if is_number(c) and c == -1:
                    split_weights(2, w12[:, 0:HIDDEN], w1_high, w1_low)
                if has_image(c + CONV - 1):
                    dve.wait_ge(normed2_rounded, c + CONV)
                    nc.vector.tensor_tensor(out=normed2_low, in0=normed2, in1=normed2_high.bitcast(fp32),
                                            op=ALU.subtract).then_inc(normed2_split, 1)
                if has_image(c):
                    output_half(c, 1)

            def output_half(c, t):
                dve.wait_ge(ffn_ready, c * NT + t + 1)
                if t == 0:
                    at_least(dve, result_out, c * 16)
                nc.vector.scalar_tensor_tensor(out=result[:, HALF * t:HALF * t + HALF], in0=psum[:, OUT_BANK, :],
                                               scalar=params[:, FFN_B2:FFN_B2 + 1], in1=image_of_x(c, HALF * t, HALF),
                                               op0=ALU.add, op1=ALU.add).then_inc(result_ready, 1)

            nc.vector.memset(neg_half, -0.5).then_inc(setup_done, 1)
            nc.vector.memset(gn_eps, GN_EPS).then_inc(setup_done, 1)
            nc.vector.memset(values[:, :, :, :, :], 1.0).then_inc(setup_done, 1)
            dve.wait_ge(weights_in, 16 * WEIGHT_DMAS)
            dve.wait_ge(setup_done, 3)
            dve.wait_ge(bias_ready, 1)
            nc.vector.tensor_tensor(out=out_bias[:, :], in0=misc[:, 0:1], in1=params[:, PROJ_B:PROJ_B + 1],
                                    op=ALU.add).then_inc(bias_taken, 1)
            dve.wait_ge(bias_taken, 1)
            nc.vector.memset(averager[:, :], 1.0 / C).then_inc(ffn_setup, 1)
            run(dve, slot, refine, activate)


def kernel(x, L0_conv_norm_w, L0_conv_norm_b, L0_conv_qkv_w, L0_conv_qkv_b, L0_conv_proj_w, L0_conv_proj_b,
           L1_conv_norm1_w, L1_conv_conv_w, L1_conv_conv_b, L1_conv_norm2_w, L1_conv_ffn_w1, L1_conv_ffn_b1,
           L1_conv_ffn_w2, L1_conv_ffn_b2):
    import numpy as np
    import concourse.bacc as bacc
    from concourse.bass_utils import run_bass_kernel_spmd

    def flat(a):
        return np.asarray(a).reshape(-1)

    qkv_w = np.asarray(L0_conv_qkv_w).reshape(2, 2, 2, 3, CH, C)
    qkv_b = np.asarray(L0_conv_qkv_b).reshape(2, 2, 2, 3, CH)
    split_w = qkv_w.transpose(3, 5, 0, 2, 4, 1).reshape(3, C, C)
    split_b = qkv_b.transpose(3, 0, 2, 4, 1).reshape(3, C)
    value_w = qkv_w[:, :, :, 2].transpose(4, 0, 1, 2, 3).reshape(C, C)
    value_b = qkv_b[:, :, :, 2].reshape(C)
    group = np.arange(C) // (C // GROUPS)
    columns = [None] * PARAMS
    for at, v in ((NORM_W, L0_conv_norm_w), (NORM_B, L0_conv_norm_b), (Q_B, split_b[0]), (K_B, split_b[1]), (V_B, value_b),
                  (PROJ_B, L0_conv_proj_b), (RMS1_W, L1_conv_norm1_w), (CONV_B, L1_conv_conv_b),
                  (RMS2_W, L1_conv_norm2_w), (FFN_B2, L1_conv_ffn_b2)):
        columns[at] = flat(v)
    for m in range(HB):
        columns[FFN_B1 + m] = flat(L1_conv_ffn_b1)[128 * m:128 * m + 128]
    arrays = {
        "x": np.asarray(x).reshape(IMAGES, C, PIXELS),
        "params": np.stack(columns, axis=1),
        "wq": split_w[0], "wk": split_w[1], "wv": value_w,
        "wp": np.asarray(L0_conv_proj_w).T,
        "group_mean": np.where(group[:, None] == group[None, :], np.float32(GROUPS / C), np.float32(0)).astype(np.float32),
        "identity": np.eye(C, dtype=np.float32),
        "wconv": np.asarray(L1_conv_conv_w).T,
        "w12": np.concatenate([np.asarray(L1_conv_ffn_w1).T, np.asarray(L1_conv_ffn_w2).reshape(C, HB, 128).transpose(
            2, 1, 0).reshape(128, HIDDEN)], axis=1),
    }
    arrays = {k: np.ascontiguousarray(v) for k, v in arrays.items()}
    nc = bacc.Bacc("TRN2", target_bir_lowering=False, num_devices=1)
    fp32 = mybir.dt.float32
    d = {k: nc.dram_tensor(f"in_{k}", v.shape, fp32, kind="ExternalInput").ap() for k, v in arrays.items()}
    d["out"] = nc.dram_tensor("out", (IMAGES, C, PIXELS), fp32, kind="ExternalOutput").ap()
    d["inv"] = nc.dram_tensor("inv_den_rows", (HEADS, PIXELS), fp32, kind="Internal").ap()
    d["rms"] = nc.dram_tensor("inv_rms_rows", (2, PIXELS), fp32, kind="Internal").ap()
    build(nc, d)
    r = run_bass_kernel_spmd(nc, [{f"in_{k}": v for k, v in arrays.items()}], core_ids=[0])
    return r.results[0]["out"].reshape(IMAGES, C, 32, 32)
```
